# Optimizing a Trainium2 kernel written in Bass

```python
import numpy as np
import jax
import jax.numpy as jnp

def _softmax(x, axis=-1):
    return jax.nn.softmax(x, axis=axis)

def _gelu(x):
    return jax.nn.gelu(x, approximate=True)

def _silu(x):
    return jax.nn.silu(x)

def _sigmoid(x):
    return jax.nn.sigmoid(x)

def _layernorm(x, axis=-1, eps=1e-05):
    m = jnp.mean(x, axis=axis, keepdims=True)
    v = jnp.var(x, axis=axis, keepdims=True)
    return (x - m) / jnp.sqrt(v + eps)

def _scatter_add(tgt, idx, src, axis=0):
    return tgt.at[idx].add(src)

def _segment_sum(src, seg, n):
    return jax.ops.segment_sum(src, seg, n)
kernel_name = 'mk_lm_tower_d1_tok_ids256_r4_63e016'

def setup_inputs(seed: int=0):
    np.random.seed(seed)
    _w = jnp.asarray

    def _rec_inputs():
        import jax
        import jax.numpy as jnp
        _rk = jax.random.key(seed)
        x = jax.random.randint(jax.random.fold_in(_rk, 1), (8, 512), 0, 24991, jnp.int32)
        return x
    x = _rec_inputs()

    def _L0_tok_setup():
        import jax, jax.numpy as jnp
        import numpy as np
        VOCAB = 25000
        EMB_DIM = 75
        OUT_DIM = 64
        B, T = (32, 128)
        key = jax.random.key(seed)
        ks = jax.random.split(key, 8)
        scale = 0.02
        return {'tokens': jax.random.randint(ks[0], (B, T), 0, VOCAB, dtype=jnp.int32), 'E0': jax.random.normal(ks[1], (VOCAB, EMB_DIM), dtype=jnp.float32) * scale, 'E1': jax.random.normal(ks[2], (VOCAB, EMB_DIM), dtype=jnp.float32) * scale, 'W0': jax.random.normal(ks[3], (EMB_DIM, OUT_DIM), dtype=jnp.float32) * scale, 'b0': jnp.zeros((OUT_DIM,), dtype=jnp.float32), 'W1': jax.random.normal(ks[4], (EMB_DIM, OUT_DIM), dtype=jnp.float32) * scale, 'b1': jnp.zeros((OUT_DIM,), dtype=jnp.float32), 'Wa': jax.random.normal(ks[5], (OUT_DIM, 1), dtype=jnp.float32) * scale, 'ba': jnp.zeros((1,), dtype=jnp.float32)}
    _L0_tok_all = _L0_tok_setup()
    _L0_tok_in = {k: v for k, v in _L0_tok_all.items() if k in ('E0', 'E1', 'W0', 'b0', 'W1', 'b1', 'Wa', 'ba')}
    del _L0_tok_all

    def _L0_attn_setup():
        import jax, jax.numpy as jnp
        import numpy as np
        from math import sqrt
        DIM = 64
        key = jax.random.key(seed)
        k1, k2, k3, k4 = jax.random.split(key, 4)
        B, T, D, H, R = (2, 1024, DIM, 8, 32)

        def xavier(k, shape, fan_in, fan_out):
            a = sqrt(6.0 / (fan_in + fan_out))
            return jax.random.uniform(k, shape, jnp.float32, -a, a)
        x = jax.random.normal(k1, (B, T, D), jnp.float32)
        Q = xavier(k2, (H, R, D), D, R)
        K = xavier(k3, (H, R, D), D, R)
        VO = xavier(k4, (H, D, D), D, D)
        return {'x': x, 'Q': Q, 'K': K, 'VO': VO}
    _L0_attn_all = _L0_attn_setup()
    _L0_attn_in = {k: v for k, v in _L0_attn_all.items() if k in ('Q', 'K', 'VO')}
    del _L0_attn_all

    def _L0_ffn_setup():
        import jax, jax.numpy as jnp
        import numpy as np
        C = 64
        HID = 256
        E = 8
        TEMP = 1.0
        key = jax.random.key(seed)
        ks = jax.random.split(key, 7)
        x = jax.random.normal(ks[0], (8, 4096, C), dtype=jnp.float32)
        W1 = jax.random.normal(ks[1], (C, HID), dtype=jnp.float32) * 0.02
        b1 = jnp.zeros((HID,), dtype=jnp.float32)
        Wg = jax.random.normal(ks[2], (HID, E), dtype=jnp.float32) * 0.02
        bg = jnp.zeros((E,), dtype=jnp.float32)
        Wd = jax.random.normal(ks[3], (E, HID, C), dtype=jnp.float32) * 0.02
        bd = jnp.zeros((E, C), dtype=jnp.float32)
        return {'x': x, 'W1': W1, 'b1': b1, 'Wg': Wg, 'bg': bg, 'Wd': Wd, 'bd': bd}
    _L0_ffn_all = _L0_ffn_setup()
    _L0_ffn_in = {k: v for k, v in _L0_ffn_all.items() if k in ('W1', 'b1', 'Wg', 'bg', 'Wd', 'bd')}
    del _L0_ffn_all
    return {'x': x, 'L0_tok_E0': _L0_tok_in['E0'], 'L0_tok_E1': _L0_tok_in['E1'], 'L0_tok_W0': _L0_tok_in['W0'], 'L0_tok_b0': _L0_tok_in['b0'], 'L0_tok_W1': _L0_tok_in['W1'], 'L0_tok_b1': _L0_tok_in['b1'], 'L0_tok_Wa': _L0_tok_in['Wa'], 'L0_tok_ba': _L0_tok_in['ba'], 'L0_attn_Q': _L0_attn_in['Q'], 'L0_attn_K': _L0_attn_in['K'], 'L0_attn_VO': _L0_attn_in['VO'], 'L0_ffn_W1': _L0_ffn_in['W1'], 'L0_ffn_b1': _L0_ffn_in['b1'], 'L0_ffn_Wg': _L0_ffn_in['Wg'], 'L0_ffn_bg': _L0_ffn_in['bg'], 'L0_ffn_Wd': _L0_ffn_in['Wd'], 'L0_ffn_bd': _L0_ffn_in['bd']}

def reference(x, L0_tok_E0, L0_tok_E1, L0_tok_W0, L0_tok_b0, L0_tok_W1, L0_tok_b1, L0_tok_Wa, L0_tok_ba, L0_attn_Q, L0_attn_K, L0_attn_VO, L0_ffn_W1, L0_ffn_b1, L0_ffn_Wg, L0_ffn_bg, L0_ffn_Wd, L0_ffn_bd):
    import jax
    import jax.numpy as jnp

    def _L0_tok_ref(tokens, E0, E1, W0, b0, W1, b1, Wa, ba):
        import jax, jax.numpy as jnp
        import numpy as np
        VOCAB = 25000
        EMB_DIM = 75
        OUT_DIM = 64
        B, T = (32, 128)
        e0 = E0[tokens]
        e1 = E1[tokens]
        p0 = jnp.einsum('bte,eo->bto', e0, W0) + b0
        p1 = jnp.einsum('bte,eo->bto', e1, W1) + b1
        projected = jnp.stack([p0, p1], axis=2)
        logits = jnp.einsum('btno,oi->btni', projected, Wa) + ba
        alphas = jax.nn.softmax(logits, axis=-2)
        out = jnp.sum(projected * alphas, axis=2)
        return out

    def _L0_attn_ref(x, Q, K, VO):
        import jax, jax.numpy as jnp
        import numpy as np
        from math import sqrt
        DIM = 64
        d = x.shape[-1]
        q = jnp.einsum('btd,hrd->bhtr', x, Q)
        k = jnp.einsum('bud,hrd->bhur', x, K)
        scores = jnp.einsum('bhtr,bhur->bhtu', q, k) / sqrt(d)
        attn = jax.nn.softmax(scores, axis=-1)
        ctx = jnp.einsum('bhtu,bud->bhtd', attn, x)
        out = jnp.einsum('bhtd,hde->bte', ctx, VO)
        return out

    def _L0_ffn_ref(x, W1, b1, Wg, bg, Wd, bd):
        import jax, jax.numpy as jnp
        import numpy as np
        C = 64
        HID = 256
        E = 8
        TEMP = 1.0
        orig_shape = x.shape
        xf = x.reshape(-1, orig_shape[-1])
        H = jax.nn.gelu(xf @ W1 + b1, approximate=False)
        probs = jax.nn.softmax((H @ Wg + bg) / TEMP, axis=-1)
        assign = jnp.argmax(probs, axis=-1)
        out = jnp.zeros_like(xf)
        for e in range(Wd.shape[0]):
            y = H @ Wd[e] + bd[e]
            sel = (assign == e)[:, None]
            out = out + jnp.where(sel, probs[:, e:e + 1] * y, 0.0)
        return out.reshape(orig_shape)
    h = _L0_tok_ref(x, L0_tok_E0, L0_tok_E1, L0_tok_W0, L0_tok_b0, L0_tok_W1, L0_tok_b1, L0_tok_Wa, L0_tok_ba)
    h = h + _L0_attn_ref(_layernorm(h, axis=-1), L0_attn_Q, L0_attn_K, L0_attn_VO)
    h = h + _L0_ffn_ref(_layernorm(h, axis=-1), L0_ffn_W1, L0_ffn_b1, L0_ffn_Wg, L0_ffn_bg, L0_ffn_Wd, L0_ffn_bd)
    return h

_drawn_inputs = setup_inputs


def setup_inputs(seed=0):
    import zlib

    import numpy as np

    out = dict(_drawn_inputs(seed))
    spreads = {'L0_tok_b0': (0.0, 0.1),
     'L0_tok_b1': (0.0, 0.1),
     'L0_ffn_b1': (0.0, 0.8),
     'L0_ffn_bg': (0.0, 0.8),
     'L0_ffn_bd': (0.0, 0.8)}
    factors = {'L0_tok_E0': 8.0,
     'L0_tok_E1': 8.0,
     'L0_tok_W0': 8.0,
     'L0_tok_W1': 8.0,
     'L0_tok_Wa': 8.0,
     'L0_attn_Q': 8.0,
     'L0_attn_K': 8.0,
     'L0_ffn_W1': 8.0,
     'L0_ffn_Wg': 8.0,
     'L0_ffn_Wd': 8.0}
    for name, (base, spread) in spreads.items():
        noise = np.random.default_rng([zlib.crc32(name.encode()), seed]).standard_normal(out[name].shape)
        drawn = base * np.exp(spread * noise) if base else spread * noise
        out[name] = jnp.asarray(drawn.astype(out[name].dtype))
    for name, factor in factors.items():
        out[name] = (out[name] * factor).astype(out[name].dtype)
    return out
```

```python
from contextlib import ExitStack

import numpy as np

import concourse.bass as bass
from concourse import mybir

FP32 = mybir.dt.float32
FP32R = mybir.dt.float32r
INT32 = mybir.dt.int32
ALU = mybir.AluOpType
ACT = mybir.ActivationFunctionType
AX = mybir.AxisListType

B, T, C = 8, 512, 64
VOCAB, EMB = 25000, 75
H, R = 8, 32
HID, NE = 256, 8
P = 128
J = T // P
HG = P // R
G = H // HG
M = HID // P
NT = H * J
GT = HG * J
LEAD = NT - 8
S_BANKS, ST_BANKS, P_BUFS = 3, 2, 4
EPS = 1e-5

SHARED = [("ctx_t", -1), ("q1", 1), ("k1", 1), ("x2_t", -1), ("hid0", -1), ("hid1", -1), ("row1", 0), ("gate", -1),
          ("y0", -1), ("y1", -1), ("y2", -1), ("y3", -1), ("v1a", 1), ("v1b", 1),
          ("e0_t", 2), ("e1_t", 2), ("proj", 2), ("proj_t", 2), ("row0", 1), ("x_t", 2),
          ("q0", 2), ("k0", 2), ("v0a", 2), ("v0b", 2)]
POS = {name: n for n, (name, _) in enumerate(SHARED)}
LINKS = {"alpha": 9, "ln1": 7, "ln2": 7, "h1": 1, "row": 4, "gate": 7}


def real(b):
    return not isinstance(b, int) or 0 <= b < B


def at_least(eng, sem, value):
    if not isinstance(value, int) or value > 0:
        eng.wait_ge(sem, value)


def lm_tower(nc, tokens, emb, W0, b0, W1, b1, Wa, ba, QT, KT, VOT, fW1, fb1, Wg, bg, WdT, bd, out):
    ctx = ExitStack()
    with ctx:
        def sb(name, shape, dt=FP32):
            return ctx.enter_context(nc.sbuf_tensor(name, shape, dt))

        def pb(name):
            return ctx.enter_context(nc.psum_tensor(name, [P, 512], FP32))

        def sem(name):
            return ctx.enter_context(nc.semaphore(name))

        ident = sb("ident", [P, P])
        emb_w = sb("emb_w", [EMB, 2, C])
        emb_b = sb("emb_b", [P, 1])
        wa = sb("wa", [P, C])
        ba_s = sb("ba_s", [P, 1])
        w_raw = sb("w_raw", [P, 256 + 256 + 512 + 256])
        w_hi = sb("w_hi", [P, 1280], FP32R)
        w_lo = sb("w_lo", [P, 1280], FP32R)
        QO, KO, VO_, FO = 0, 256, 512, 1024
        fb1_s = sb("fb1_s", [P, M])
        wg = sb("wg", [P, M, NE])
        bg_s = sb("bg_s", [P, NE])
        wd = sb("wd", [P, M, NE * C])
        bd_s = sb("bd_s", [P, NE * C])
        rank = sb("rank", [P, NE])
        half = sb("half", [P, J])

        idx = sb("idx", [P, J], INT32)
        rows = sb("rows", [P, J, 2 * EMB])
        rows_t = sb("rows_t", [EMB, 2, T])
        proj = sb("proj", [P, T])
        lw = sb("lw", [P, J * 2, C])
        logit = sb("logit", [P, J, 2])
        lmax = sb("lmax", [P, J])
        alpha = sb("alpha", [P, J, 2])
        lsum = sb("lsum", [P, J])
        h_now = sb("h_now", [P, J, C])
        h_all = sb("h_all", [P, B, J * C])
        mean = [sb(f"mean{n}", [P, J]) for n in range(2)]
        cent = [sb(f"cent{n}", [P, J, C]) for n in range(2)]
        sq = [sb(f"sq{n}", [P, J, C]) for n in range(2)]
        var = [sb(f"var{n}", [P, J]) for n in range(2)]
        rstd = [sb(f"rstd{n}", [P, J]) for n in range(2)]
        xs = [sb(f"xs{n}", [P, J, 2 * C], FP32R) for n in range(2)]
        xt = [sb(f"xt{n}", [P, T], FP32R) for n in range(2)]
        raw_q = [sb(f"raw_q{g}", [P, 2, T], FP32R) for g in range(G)]
        raw_k = [sb(f"raw_k{g}", [P, 2, T], FP32R) for g in range(G)]
        raw_v = [sb(f"raw_v{g}", [P, J, HG * C]) for g in range(G)]
        full_q = sb("full_q", [P, T])
        qst = sb("qst", [3 * R + 2, H, T], FP32R)
        kst = sb("kst", [3 * R + 2, H, T], FP32R)
        val = sb("val", [P, H, J, C])
        neg_max = sb("neg_max", [P, NT])
        den = sb("den", [P, NT])
        ln_den = sb("ln_den", [P, NT])
        shift = sb("shift", [P, J, HG])
        shift_s = sb("shift_s", [P, J, 2, HG], FP32R)
        shift_t = sb("shift_t", [2 * HG, T], FP32R)
        prob = sb("prob", [P, P_BUFS, T])
        ctx_s = sb("ctx_s", [P, T])
        h1 = sb("h1", [P, J, C])
        hid = sb("hid", [P, M, T])
        gl = sb("gl", [P, J, NE])
        gmax = sb("gmax", [P, J])
        gd = sb("gd", [P, J, NE])
        ge = sb("ge", [P, J, NE])
        gsum = sb("gsum", [P, J])
        gp = sb("gp", [P, J])
        geq = sb("geq", [P, J, NE])
        gtop = sb("gtop", [P, J])
        coef = sb("coef", [P, J, NE])
        yb = sb("yb", [P, 2, NE, C])
        yc = sb("yc", [P, NE, C])
        res = sb("res", [P, J, C])

        s_ps = [pb(f"s_ps{n}") for n in range(S_BANKS)]
        st_ps = [pb(f"st_ps{n}") for n in range(ST_BANKS)]
        ctx_ps = pb("ctx_ps")
        sh_ps = [pb(f"sh_ps{n}") for n in range(2)]

        def bank(name):
            return sh_ps[POS[name] % 2]

        w_loaded, w_split, const_ready = sem("w_loaded"), sem("w_split"), sem("const_ready")
        idx_loaded, rows_loaded, rows_free = sem("idx_loaded"), sem("rows_loaded"), sem("rows_free")
        filled = {name: sem(f"filled_{name}") for name, _ in SHARED}
        emptied = {name: sem(f"emptied_{name}") for name, _ in SHARED}
        alpha_in, alpha_exp = sem("alpha_in"), sem("alpha_exp")
        var_ready = [sem(f"var_ready{n}") for n in range(2)]
        rstd_ready = [sem(f"rstd_ready{n}") for n in range(2)]
        xs_ready = [sem(f"xs_ready{n}") for n in range(2)]
        stacked = [sem(f"stacked{h}") for h in range(H)]
        v_stored = [sem(f"v_stored{h}") for h in range(H)]
        s_done, max_done, s_exp = sem("s_done"), sem("max_done"), sem("s_exp")
        ln_done, shift_ready = sem("ln_done"), sem("shift_ready")
        shift_stored = [sem(f"shift_stored{g}") for g in range(G)]
        st_done, p_done, pv_done = sem("st_done"), sem("p_done"), sem("pv_done")
        ctx_read = sem("ctx_read")
        gate_in, gate_exp, coef_ready = sem("gate_in"), sem("gate_exp"), sem("coef_ready")
        y_used, res_ready, out_stored = sem("y_used"), sem("res_ready"), sem("out_stored")
        pool_step = sem("pool_step")
        pool_turn, sync_turn = sem("pool_turn"), sem("sync_turn")
        link_sem = {name: sem(f"link_{name}") for name in LINKS}
        STACK = 6 * 16
        N_W = 12 * 16 + 16 * 4

        block = ctx.enter_context(nc.Block())

        def s_tile(i, t):
            return (i, t + LEAD) if t < NT - LEAD else (i + 1, t + LEAD - NT)

        def lagged(i, t):
            return s_tile(i, t - 1) if t else (i, LEAD - 1)

        def wait_sync(sp, sema, value):
            at_least(sp, sema, value)
            if not isinstance(value, int):
                sp.sem_inc(sync_turn, 1)

        def load_idx(sp, b):
            wait_sync(sp, rows_loaded, 16 * J * b)
            sp.dma_start(idx[:, :], tokens[b, :].rearrange("(p j) -> p j", j=J)).then_inc(idx_loaded, 16)

        def stack_head(sp, b, h):
            g, r = h // HG, (h % HG) * R
            wait_sync(sp, emptied[f"q{g}"], b + 1)
            wait_sync(sp, emptied[f"k{g}"], b + 1)
            wait_sync(sp, st_done, NT * (b - 1) + J * (h + 1))
            for dst, src, slot, part in ((qst, raw_q, 0, 0), (qst, raw_q, 1, 0), (qst, raw_q, 2, 1),
                                         (kst, raw_k, 0, 0), (kst, raw_k, 1, 1), (kst, raw_k, 2, 0)):
                sp.dma_start(dst[slot * R:(slot + 1) * R, h, :].bitcast(FP32), src[g][r:r + R, part, :].bitcast(FP32)).then_inc(stacked[h], 16)

        def store_v(sp, b, h):
            g = h // HG
            wait_sync(sp, emptied[f"v{g}a"], b + 1)
            wait_sync(sp, emptied[f"v{g}b"], b + 1)
            wait_sync(sp, pv_done, NT // 2 * (b - 1) + J // 2 * (h + 1))
            c0 = (h % HG) * C
            sp.dma_start(val[:, h, :, :], raw_v[g][:, :, c0:c0 + C]).then_inc(v_stored[h], 16)

        def store_shift(sp, b, g):
            wait_sync(sp, emptied[f"row{g}"], b + 1)
            for part in range(2):
                sp.dma_start(qst[3 * R + part:3 * R + part + 1, g * HG:(g + 1) * HG, :].bitcast(FP32),
                             shift_t[part * HG:(part + 1) * HG, :].bitcast(FP32)).then_inc(shift_stored[g], 16)

        def store_out(sp, b):
            wait_sync(sp, res_ready, J * (b + 1))
            sp.dma_start(out[b, :, :].rearrange("(p j) c -> p (j c)", j=J), res[:, :, :].rearrange("p j c -> p (j c)")).then_inc(out_stored, 16)

        def sync_body(sp, i):
            for t in range(NT):
                if t == 2 and real(i):
                    store_v(sp, i, H - 1)
                if t % J == J - 1 and real(i + 1):
                    stack_head(sp, i + 1, t // J)
                if t % J == 2 and t >= 6 and real(i + 1):
                    store_v(sp, i + 1, t // J - 1)
                if t == 12 and real(i):
                    store_shift(sp, i, 1)
                if t == 0 and real(i + 2):
                    load_idx(sp, i + 2)
                if t == 21 and real(i - 1):
                    store_out(sp, i - 1)
                if t == 28 and real(i + 1):
                    store_shift(sp, i + 1, 0)

        @block.sync
        def _(sp):
            sp.sem_inc(out_stored, 16)
            for half_ in range(2):
                p = slice(half_ * C, (half_ + 1) * C)
                for off, src in ((QO, QT), (KO, KT), (VO_, VOT), (FO, fW1)):
                    sp.dma_start(w_raw[p, off:off + src.shape[1]], src).then_inc(w_loaded, 16)
            sp.dma_start(emb_w[:, 0, :], W0).then_inc(w_loaded, 16)
            sp.dma_start(emb_w[:, 1, :], W1).then_inc(w_loaded, 16)
            sp.dma_start(emb_b[0:C, :], b0).then_inc(w_loaded, 16)
            sp.dma_start(emb_b[C:P, :], b1).then_inc(w_loaded, 16)
            sp.dma_start(wa[:, :], Wa.to_broadcast([P, C])).then_inc(w_loaded, 16)
            sp.dma_start(ba_s[:, :], ba.to_broadcast([P, 1])).then_inc(w_loaded, 16)
            sp.dma_start(fb1_s[:, :], fb1).then_inc(w_loaded, 16)
            sp.dma_start(wg[:, :, :], Wg.rearrange("(m p) e -> p m e", p=P)).then_inc(w_loaded, 16)
            sp.dma_start(bg_s[:, :], bg.to_broadcast([P, NE])).then_inc(w_loaded, 16)
            sp.dma_start(wd[:, :, :], WdT.rearrange("(m p) f -> p m f", p=P)).then_inc(w_loaded, 16)
            sp.dma_start(bd_s[:, :], bd.to_broadcast([P, NE * C])).then_inc(w_loaded, 16)
            for i in (-2, -1, 0):
                sync_body(sp, i)
            with sp.Fori(1, B - 2) as i:
                sync_body(sp, i)
            for i in (B - 2, B - 1, B):
                sync_body(sp, i)
            sp.wait_ge(out_stored, 16 * (B + 1))

        W_ALL = 16 * (8 + 11)

        def gather(pool, b):
            at_least(pool, idx_loaded, 16 * (b + 1))
            at_least(pool, filled["e1_t"], b)
            pool.sem_inc(pool_turn, 1)
            for j in range(J):
                nc.gpsimd.indirect_dma_start(out=rows[:, j, :], out_offset=None, in_=emb,
                                             in_offset=bass.IndirectOffsetOnAxis(ap=idx[:, j:j + 1], axis=0)
                                             ).then_inc(rows_loaded, 16)

        def inverse_std(pool, b, n):
            at_least(pool, var_ready[n], b + 1)
            nc.gpsimd.tensor_tensor(rstd[n][:, :], var[n][:, :], half[:, :], ALU.pow).then_inc(rstd_ready[n], 1)

        def mix(pool, b, j):
            at_least(pool, emptied[f"y{j}"], b + 1)
            at_least(pool, coef_ready, b + 1)
            k = 4 * (J * b + j)
            if j:
                at_least(pool, res_ready, J * b + j)
            nc.gpsimd.tensor_tensor(yc[:, :, :], yb[:, j % 2, :, :], coef[:, j, :].unsqueeze(2).to_broadcast([P, NE, C]),
                                    ALU.mult).then_inc(pool_step, 1)
            pool.wait_ge(pool_step, k + 1)
            nc.gpsimd.tensor_tensor(yc[:, 0:4, :], yc[:, 0:4, :], yc[:, 4:8, :], ALU.add).then_inc(pool_step, 1)
            pool.wait_ge(pool_step, k + 2)
            nc.gpsimd.tensor_tensor(yc[:, 0:2, :], yc[:, 0:2, :], yc[:, 2:4, :], ALU.add).then_inc(pool_step, 1)
            pool.wait_ge(pool_step, k + 3)
            nc.gpsimd.tensor_tensor(yc[:, 0, :], yc[:, 0, :], yc[:, 1, :], ALU.add).then_inc(pool_step, 1)
            pool.wait_ge(pool_step, k + 4)
            nc.gpsimd.tensor_tensor(res[:, j, :], yc[:, 0, :], h1[:, j, :], ALU.add).then_inc(res_ready, 1)

        def pool_body(pool, i):
            if real(i + 2):
                gather(pool, i + 2)
            if real(i - 1):
                inverse_std(pool, i - 1, 1)
                for j in range(J):
                    mix(pool, i - 1, j)
            if real(i + 2):
                inverse_std(pool, i + 2, 0)

        @block.gpsimd
        def _(pool):
            nc.gpsimd.memset(ident[:, :], 0.0).then_inc(const_ready, 1)
            pool.wait_ge(const_ready, 1)
            nc.gpsimd.affine_select(out=ident[:, :], in_=ident[:, :], compare_op=ALU.not_equal, fill=1.0, base=0,
                                    pattern=[[-1, P]], channel_multiplier=1).then_inc(const_ready, 1)
            nc.gpsimd.iota(rank[:, :], pattern=[[-1, NE]], base=NE, channel_multiplier=0,
                           allow_small_or_imprecise_dtypes=True).then_inc(const_ready, 1)
            nc.gpsimd.memset(half[:, :], -0.5).then_inc(const_ready, 1)
            pool.wait_ge(const_ready, 4)
            nc.gpsimd.memset(kst[3 * R:3 * R + 2, :, :].bitcast(FP32), 1.0).then_inc(const_ready, 1)
            pool.wait_ge(const_ready, 5)
            for i in (-2, -1, 0):
                pool_body(pool, i)
            with pool.Fori(1, B - 2) as i:
                pool_body(pool, i)
            for i in (B - 2, B - 1, B):
                pool_body(pool, i)

        def exp_scores(act, b, n):
            at_least(act, max_done, NT * b + n + 1)
            ps = s_ps[n % S_BANKS]
            nc.scalar.activation(ps[:, :], ps[:, :], ACT.Exp, bias=neg_max[:, n:n + 1], scale=-1.0,
                                 accum_out=den[:, n:n + 1]).then_inc(s_exp, 1)

        def exp_probs(act, b, n):
            at_least(act, st_done, NT * b + n + 1)
            at_least(act, pv_done, NT // 2 * b + n // 2 - 1)
            nc.scalar.activation(prob[:, n % P_BUFS, :], st_ps[n % ST_BANKS][:, :], ACT.Exp, scale=-1.0).then_inc(p_done, 1)

        def log_sum(act, b, g):
            at_least(act, s_exp, NT * b + GT * (g + 1))
            nc.scalar.activation(ln_den[:, GT * g:GT * (g + 1)], den[:, GT * g:GT * (g + 1)], ACT.Ln).then_inc(ln_done, 1)

        def alpha_weights(act, b):
            at_least(act, alpha_in, b + 1)
            nc.scalar.activation(alpha[:, :, :], logit[:, :, :], ACT.Exp).then_inc(alpha_exp, 1)

        def gate_weights(act, b):
            at_least(act, gate_in, b + 1)
            nc.scalar.activation(ge[:, :, :], gd[:, :, :], ACT.Exp).then_inc(gate_exp, 1)

        def gelu(act, b, m):
            at_least(act, filled[f"hid{m}"], b + 1)
            nc.scalar.activation(hid[:, m, :], bank(f"hid{m}")[:, :], ACT.Gelu, bias=fb1_s[:, m:m + 1]).then_inc(emptied[f"hid{m}"], 1)

        def act_body(act, i):
            for t in range(NT):
                b, n = lagged(i, t)
                if real(b):
                    exp_scores(act, b, n)
                if real(i):
                    exp_probs(act, i, t)
                if t == 9 and real(i):
                    log_sum(act, i, 1)
                if t == 10 and real(i - 1):
                    for m in range(M):
                        gelu(act, i - 1, m)
                if t == 13 and real(i - 1):
                    gate_weights(act, i - 1)
                if t == 24 and real(i + 2):
                    alpha_weights(act, i + 2)
                if t == 25 and real(i + 1):
                    log_sum(act, i + 1, 0)

        @block.scalar
        def _(act):
            act.preload_act_table_set("natural_log_exp_and_others")
            act.wait_ge(w_loaded, W_ALL)
            for i in (-2, -1, 0):
                act_body(act, i)
            with act.Fori(1, B - 2) as i:
                act_body(act, i)
            for i in (B - 2, B - 1, B):
                act_body(act, i)

        def links(dve, name, b):
            count = [0]

            def link(ins):
                count[0] += 1
                ins.then_inc(link_sem[name], 1)
                dve.wait_ge(link_sem[name], LINKS[name] * b + count[0])
                assert count[0] <= LINKS[name]
            return link

        V = nc.vector

        def wide(small, n):
            return small.unsqueeze(2).to_broadcast([P, J, n])

        def row_max(dve, b, n):
            at_least(dve, s_done, NT * b + n + 1)
            V.tensor_reduce(neg_max[:, n:n + 1], s_ps[n % S_BANKS][:, :], AX.X, ALU.min).then_inc(max_done, 1)

        def rows_out(dve, b):
            for n in range(2):
                at_least(dve, filled[f"e{n}_t"], b + 1)
                V.tensor_copy(rows_t[:, n, :], bank(f"e{n}_t")[0:EMB, :]).then_inc(emptied[f"e{n}_t"], 1)

        def proj_out(dve, b):
            at_least(dve, filled["proj"], b + 1)
            V.tensor_scalar(proj[:, :], bank("proj")[:, :], emb_b[:, 0:1], None, ALU.add).then_inc(emptied["proj"], 1)

        def mix_embeddings(dve, b):
            link = links(dve, "alpha", b)
            at_least(dve, filled["proj_t"], b + 1)
            ps = bank("proj_t")[:, :].rearrange("p (k c) -> p k c", c=C)
            lflat = logit[:, :, :].rearrange("p j n -> p (j n)")
            link(V.tensor_tensor(lw[:, :, :], ps, wa[:, :].unsqueeze(1).to_broadcast([P, 2 * J, C]), ALU.mult))
            link(V.tensor_reduce(lflat, lw[:, :, :], AX.X, ALU.add))
            link(V.tensor_scalar(lflat, lflat, ba_s[:, 0:1], None, ALU.add))
            link(V.tensor_reduce(lmax[:, :], logit[:, :, :], AX.X, ALU.max))
            V.tensor_tensor(logit[:, :, :], logit[:, :, :], wide(lmax[:, :], 2), ALU.subtract).then_inc(alpha_in, 1)
            at_least(dve, alpha_exp, b + 1)
            link(V.tensor_reduce(lsum[:, :], alpha[:, :, :], AX.X, ALU.add))
            link(V.reciprocal(lsum[:, :], lsum[:, :]))
            link(V.tensor_tensor(alpha[:, :, :], alpha[:, :, :], wide(lsum[:, :], 2), ALU.mult))
            aflat = alpha[:, :, :].rearrange("p j n -> p (j n)").unsqueeze(2).to_broadcast([P, 2 * J, C])
            V.tensor_tensor(lw[:, :, :], ps, aflat, ALU.mult).then_inc(emptied["proj_t"], 1)
            at_least(dve, emptied["proj_t"], b + 1)
            w4 = lw[:, :, :].rearrange("p (j n) c -> p j n c", n=2)
            h_b = h_all[:, b, :].rearrange("p (j c) -> p j c", c=C)
            link(V.tensor_tensor(h_b, w4[:, :, 0, :], w4[:, :, 1, :], ALU.add))
            link(V.tensor_tensor(h_now[:, :, :], w4[:, :, 0, :], w4[:, :, 1, :], ALU.add))
            layer_norm(dve, b, 0, h_now[:, :, :])

        def layer_norm(dve, b, n, x):
            link = links(dve, f"ln{n + 1}", b)
            link(V.tensor_reduce(mean[n][:, :], x, AX.X, ALU.add))
            link(V.tensor_scalar(mean[n][:, :], mean[n][:, :], 1.0 / C, None, ALU.mult))
            link(V.tensor_tensor(cent[n][:, :, :], x, wide(mean[n][:, :], C), ALU.subtract))
            link(V.tensor_tensor(sq[n][:, :, :], cent[n][:, :, :], cent[n][:, :, :], ALU.mult))
            link(V.tensor_reduce(var[n][:, :], sq[n][:, :, :], AX.X, ALU.add))
            V.tensor_scalar(var[n][:, :], var[n][:, :], 1.0 / C, EPS, ALU.mult, ALU.add).then_inc(var_ready[n], 1)
            at_least(dve, rstd_ready[n], b + 1)
            link(V.tensor_tensor(sq[n][:, :, :], cent[n][:, :, :], wide(rstd[n][:, :], C), ALU.mult))
            link(V.tensor_copy(xs[n][:, :, 0:C], sq[n][:, :, :]))
            V.tensor_tensor(xs[n][:, :, C:2 * C], sq[n][:, :, :], xs[n][:, :, 0:C].bitcast(FP32), ALU.subtract).then_inc(xs_ready[n], 1)

        def x_out(dve, b, n):
            name = ("x_t", "x2_t")[n]
            at_least(dve, filled[name], b + 1)
            V.tensor_copy(xt[n][:, :], bank(name)[:, :]).then_inc(emptied[name], 1)

        def split_qk(dve, b, g, which):
            name = f"{which}{g}"
            raw, scale = (raw_q, -1.0 / C ** 0.5) if which == "q" else (raw_k, 1.0)
            at_least(dve, filled[name], b + 1)
            if which == "q":
                for h in range(g * HG, (g + 1) * HG):
                    at_least(dve, stacked[h], STACK * b)
            ps = bank(name)[:, :]
            V.tensor_scalar(raw[g][:, 0, :], ps, scale, None, ALU.mult).then_inc(emptied[name + "_hi"], 1)
            dve.wait_ge(emptied[name + "_hi"], b + 1)
            V.scalar_tensor_tensor(raw[g][:, 1, :], ps, scale, raw[g][:, 0, :].bitcast(FP32), ALU.mult, ALU.subtract).then_inc(emptied[name], 1)

        for which in "qk":
            for g in range(G):
                emptied[f"{which}{g}_hi"] = sem(f"high_{which}{g}")

        def v_out(dve, b, g, part):
            name = f"v{g}" + "ab"[part]
            at_least(dve, filled[name], b + 1)
            if part == 0:
                for h in range(g * HG, (g + 1) * HG):
                    at_least(dve, v_stored[h], 16 * b)
            V.tensor_copy(raw_v[g][:, 2 * part:2 * part + 2, :].rearrange("p j c -> p (j c)"), bank(name)[:, :]).then_inc(emptied[name], 1)

        def shift_parts(dve, b, g):
            at_least(dve, ln_done, G * b + g + 1)
            cols = slice(GT * g, GT * (g + 1))
            ld = ln_den[:, cols].rearrange("p (h j) -> p j h", j=J)
            nm = neg_max[:, cols].rearrange("p (h j) -> p j h", j=J)
            V.tensor_tensor(shift[:, :, :], ld, nm, ALU.subtract).then_inc(link_sem["row"], 1)
            dve.wait_ge(link_sem["row"], 4 * b + 2 * g + 1)
            V.tensor_copy(shift_s[:, :, 0, :], shift[:, :, :]).then_inc(link_sem["row"], 1)
            dve.wait_ge(link_sem["row"], 4 * b + 2 * g + 2)
            V.tensor_tensor(shift_s[:, :, 1, :], shift[:, :, :], shift_s[:, :, 0, :].bitcast(FP32), ALU.subtract).then_inc(shift_ready, 1)

        def shift_out(dve, b, g):
            at_least(dve, filled[f"row{g}"], b + 1)
            if g == 0:
                at_least(dve, shift_stored[1], 32 * b)
            else:
                at_least(dve, shift_stored[0], 32 * (b + 1))
            V.tensor_copy(shift_t[:, :], bank(f"row{g}")[0:2 * HG, :]).then_inc(emptied[f"row{g}"], 1)

        def ctx_out(dve, b):
            at_least(dve, pv_done, NT // 2 * (b + 1))
            V.tensor_copy(ctx_s[:, :], ctx_ps[:, :]).then_inc(ctx_read, 1)

        def add_attention(dve, b):
            link = links(dve, "h1", b)
            at_least(dve, filled["ctx_t"], b + 1)
            ps = bank("ctx_t")[:, :].rearrange("p (j c) -> p j c", j=J)
            h_b = h_all[:, b, :].rearrange("p (j c) -> p j c", c=C)
            dve.wait_ge(out_stored, 16 * (b + 1))
            link(V.tensor_tensor(h1[:, :, :], ps[:, :, 0:C], h_b, ALU.add))
            V.tensor_tensor(h1[:, :, :], ps[:, :, C:2 * C], h1[:, :, :], ALU.add).then_inc(emptied["ctx_t"], 1)
            at_least(dve, emptied["ctx_t"], b + 1)
            layer_norm(dve, b, 1, h1[:, :, :])

        def route(dve, b):
            link = links(dve, "gate", b)
            at_least(dve, filled["gate"], b + 1)
            ps = bank("gate")[:, 0:J * NE].rearrange("p (j e) -> p j e", e=NE)
            V.tensor_tensor(gl[:, :, :], ps, bg_s[:, :].unsqueeze(1).to_broadcast([P, J, NE]), ALU.add).then_inc(emptied["gate"], 1)
            at_least(dve, emptied["gate"], b + 1)
            link(V.tensor_reduce(gmax[:, :], gl[:, :, :], AX.X, ALU.max))
            V.tensor_tensor(gd[:, :, :], gl[:, :, :], wide(gmax[:, :], NE), ALU.subtract).then_inc(gate_in, 1)
            at_least(dve, gate_in, b + 1)
            link(V.tensor_scalar(geq[:, :, :], gd[:, :, :], 0.0, None, ALU.is_ge))
            link(V.tensor_tensor(geq[:, :, :], geq[:, :, :], rank[:, :].unsqueeze(1).to_broadcast([P, J, NE]), ALU.mult))
            link(V.tensor_reduce(gtop[:, :], geq[:, :, :], AX.X, ALU.max))
            link(V.tensor_tensor(geq[:, :, :], geq[:, :, :], wide(gtop[:, :], NE), ALU.is_equal))
            at_least(dve, gate_exp, b + 1)
            link(V.tensor_reduce(gsum[:, :], ge[:, :, :], AX.X, ALU.add))
            link(V.reciprocal(gp[:, :], gsum[:, :]))
            V.tensor_tensor(coef[:, :, :], geq[:, :, :], wide(gp[:, :], NE), ALU.mult).then_inc(coef_ready, 1)

        def y_out(dve, b, j):
            at_least(dve, filled[f"y{j}"], b + 1)
            if j >= 2:
                at_least(dve, res_ready, J * b + j - 1)
            V.tensor_tensor(yb[:, j % 2, :, :].rearrange("p e c -> p (e c)"), bank(f"y{j}")[:, :], bd_s[:, :], ALU.add).then_inc(emptied[f"y{j}"], 1)

        def vector_body(dve, i):
            for t in range(NT):
                b, n = s_tile(i, t)
                if real(b):
                    row_max(dve, b, n)
                if real(i - 1):
                    if t == 1:
                        ctx_out(dve, i - 1)
                    if t == 4:
                        add_attention(dve, i - 1)
                    if t == 8:
                        x_out(dve, i - 1, 1)
                    if t == 12:
                        route(dve, i - 1)
                    if 13 <= t < 13 + J:
                        y_out(dve, i - 1, t - 13)
                if real(i):
                    if t == 10:
                        shift_parts(dve, i, 1)
                    if t == 11:
                        shift_out(dve, i, 1)
                if real(i + 1):
                    if t == 6:
                        split_qk(dve, i + 1, 1, "q")
                    if t == 7:
                        split_qk(dve, i + 1, 1, "k")
                    if t in (17, 18):
                        v_out(dve, i + 1, 1, t - 17)
                    if t == 26:
                        shift_parts(dve, i + 1, 0)
                    if t == 27:
                        shift_out(dve, i + 1, 0)
                if real(i + 2):
                    if t == 20:
                        rows_out(dve, i + 2)
                    if t == 22:
                        proj_out(dve, i + 2)
                    if t == 24:
                        mix_embeddings(dve, i + 2)
                    if t == 28:
                        x_out(dve, i + 2, 0)
                    if t == 29:
                        split_qk(dve, i + 2, 0, "q")
                    if t == 30:
                        split_qk(dve, i + 2, 0, "k")
                    if t == 31:
                        v_out(dve, i + 2, 0, 0)
                        v_out(dve, i + 2, 0, 1)

        @block.vector
        def _(dve):
            dve.wait_ge(w_loaded, W_ALL)
            V.tensor_copy(w_hi[:, :], w_raw[:, :]).then_inc(w_split, 1)
            dve.wait_ge(w_split, 1)
            V.tensor_tensor(w_lo[:, :], w_raw[:, :], w_hi[:, :].bitcast(FP32), ALU.subtract).then_inc(w_split, 1)
            dve.wait_ge(const_ready, 5)
            for i in (-2, -1, 0):
                vector_body(dve, i)
            with dve.Fori(1, B - 2) as i:
                vector_body(dve, i)
            for i in (B - 2, B - 1, B):
                vector_body(dve, i)

        PE = nc.tensor

        def claim(pe, i, name):
            at = POS[name] - 2
            body = i
            for _ in range(3 * len(SHARED)):
                if at < 0:
                    at += len(SHARED)
                    body = body - 1
                prev, rel = SHARED[at]
                if isinstance(body + rel, int) and body + rel < 0 and body < -3:
                    return
                if real(body + rel):
                    at_least(pe, emptied[prev], body + rel + 1)
                    return
                at -= 2

        def scores(pe, b, n):
            h, c = divmod(n, J)
            if c == 0:
                pe.wait_ge(stacked[h], STACK * (b + 1))
            if n < S_BANKS:
                last = max(m for m in range(NT) if m % S_BANKS == n)
                at_least(pe, s_exp, NT * (b - 1) + last + 1)
            else:
                at_least(pe, s_exp, NT * b + n - S_BANKS + 1)
            PE.matmul(s_ps[n % S_BANKS][:, :], qst[0:3 * R, h, c * P:(c + 1) * P], kst[0:3 * R, h, :],
                      start=True, stop=True).then_inc(s_done, 1)

        def scores_t(pe, b, n):
            h, c = divmod(n, J)
            if n % GT == 0:
                pe.wait_ge(shift_stored[n // GT], 32 * (b + 1))
            at_least(pe, p_done, NT * b + n - ST_BANKS + 1)
            PE.matmul(st_ps[n % ST_BANKS][:, :], kst[:, h, c * P:(c + 1) * P], qst[:, h, :],
                      start=True, stop=True).then_inc(st_done, 1)

        def context(pe, b, pair):
            h, c = divmod(2 * pair, J)
            if c == 0:
                pe.wait_ge(v_stored[h], 16 * (b + 1))
            if pair == 0:
                at_least(pe, ctx_read, b)
            pe.wait_ge(p_done, NT * b + 2 * pair + 2)
            for d in range(2):
                last = PE.matmul(ctx_ps[d * C:(d + 1) * C, :], val[:, h, c + d, :], prob[:, (2 * pair + d) % P_BUFS, :],
                                 start=(pair == 0), stop=(pair == NT // 2 - 1))
            last.then_inc(pv_done, 1)

        def transposes(pe, i, name, pieces, rows_):
            claim(pe, i, name)
            for j, piece in enumerate(pieces):
                last = PE.transpose(bank(name)[0:rows_, j * P:(j + 1) * P], piece, ident[:, :])
            last.then_inc(filled[name], 1)

        def embed_t(pe, i, b):
            at_least(pe, rows_loaded, 16 * J * (b + 1))
            for n in range(2):
                transposes(pe, i, f"e{n}_t", [rows[:, j, n * EMB:(n + 1) * EMB] for j in range(J)], EMB)

        def embed_proj(pe, i, b):
            claim(pe, i, "proj")
            for n in range(2):
                at_least(pe, emptied[f"e{n}_t"], b + 1)
                last = PE.matmul(bank("proj")[n * C:(n + 1) * C, :], emb_w[:, n, :], rows_t[:, n, :], start=True, stop=True)
            last.then_inc(filled["proj"], 1)

        def two_pass(out_ap, parts, moving, off=None):
            PE.matmul(out_ap, parts[0], moving, start=True, stop=False)
            return PE.matmul(out_ap, parts[1], moving, start=False, stop=True)

        def project_qk(pe, i, b, g, which):
            name = f"{which}{g}"
            claim(pe, i, name)
            at_least(pe, emptied["x_t"], b + 1)
            o = (QO if which == "q" else KO) + g * P
            two_pass(bank(name)[:, :], (w_hi[:, o:o + P], w_lo[:, o:o + P]), xt[0][:, :]).then_inc(filled[name], 1)

        def project_v(pe, i, b, g, part):
            name = f"v{g}" + "ab"[part]
            claim(pe, i, name)
            at_least(pe, emptied["x_t"], b + 1)
            o = VO_ + g * HG * C
            for d in range(2):
                tok = slice((2 * part + d) * P, (2 * part + d + 1) * P)
                dst = bank(name)[:, d * HG * C:(d + 1) * HG * C]
                PE.matmul(dst, xt[0][:, tok], w_hi[:, o:o + HG * C], start=True, stop=False)
                last = PE.matmul(dst, xt[0][:, tok], w_lo[:, o:o + HG * C], start=False, stop=True)
            last.then_inc(filled[name], 1)

        def shift_row(pe, i, b, g):
            at_least(pe, shift_ready, G * b + g + 1)
            transposes(pe, i, f"row{g}", [shift_s[:, j, :, :].bitcast(FP32).rearrange("p a h -> p (a h)") for j in range(J)], 2 * HG)

        def hidden(pe, i, b, m):
            name = f"hid{m}"
            claim(pe, i, name)
            at_least(pe, emptied["x2_t"], b + 1)
            o = FO + m * P
            two_pass(bank(name)[:, :], (w_hi[:, o:o + P], w_lo[:, o:o + P]), xt[1][:, :]).then_inc(filled[name], 1)

        def gate(pe, i, b):
            claim(pe, i, "gate")
            for m in range(M):
                at_least(pe, emptied[f"hid{m}"], b + 1)
            for j in range(J):
                for m in range(M):
                    last = PE.matmul(bank("gate")[:, j * NE:(j + 1) * NE], hid[:, m, j * P:(j + 1) * P], wg[:, m, :],
                                     start=(m == 0), stop=(m == M - 1))
            last.then_inc(filled["gate"], 1)

        def experts(pe, i, b, j):
            name = f"y{j}"
            claim(pe, i, name)
            for m in range(M):
                last = PE.matmul(bank(name)[:, :], hid[:, m, j * P:(j + 1) * P], wd[:, m, :], start=(m == 0), stop=(m == M - 1))
            last.then_inc(filled[name], 1)

        def tensor_body(pe, i):
            for t in range(NT):
                b, n = s_tile(i, t)
                if real(b):
                    scores(pe, b, n)
                if real(i):
                    scores_t(pe, i, t)
                if t == 0 and real(i - 1):
                    context(pe, i - 1, NT // 2 - 1)
                if t % 2 == 0 and t >= 2 and real(i):
                    context(pe, i, t // 2 - 1)
                if real(i - 1):
                    if t == 3:
                        at_least(pe, ctx_read, i)
                        transposes(pe, i, "ctx_t", [ctx_s[:, j * P:(j + 1) * P] for j in range(J)], P)
                    if t == 7:
                        at_least(pe, xs_ready[1], i)
                        transposes(pe, i, "x2_t", [xs[1][:, j, :].bitcast(FP32) for j in range(J)], P)
                    if t in (8, 9):
                        hidden(pe, i, i - 1, t - 8)
                    if t == 11:
                        gate(pe, i, i - 1)
                    if 12 <= t < 12 + J:
                        experts(pe, i, i - 1, t - 12)
                if real(i) and t == 10:
                    shift_row(pe, i, i, 1)
                if real(i + 1):
                    if t == 5:
                        project_qk(pe, i, i + 1, 1, "q")
                    if t == 6:
                        project_qk(pe, i, i + 1, 1, "k")
                    if t in (16, 17):
                        project_v(pe, i, i + 1, 1, t - 16)
                    if t == 26:
                        shift_row(pe, i, i + 1, 0)
                if real(i + 2):
                    if t == 19:
                        embed_t(pe, i, i + 2)
                    if t == 21:
                        embed_proj(pe, i, i + 2)
                    if t == 23:
                        at_least(pe, emptied["proj"], i + 3)
                        transposes(pe, i, "proj_t", [proj[:, j * P:(j + 1) * P] for j in range(J)], P)
                    if t == 27:
                        at_least(pe, xs_ready[0], i + 3)
                        transposes(pe, i, "x_t", [xs[0][:, j, :].bitcast(FP32) for j in range(J)], P)
                    if t == 28:
                        project_qk(pe, i, i + 2, 0, "q")
                    if t == 29:
                        project_qk(pe, i, i + 2, 0, "k")
                    if t in (30, 31):
                        project_v(pe, i, i + 2, 0, t - 30)

        @block.tensor
        def _(pe):
            pe.wait_ge(const_ready, 5)
            pe.wait_ge(w_split, 2)
            for i in (-2, -1, 0):
                tensor_body(pe, i)
            with pe.Fori(1, B - 2) as i:
                tensor_body(pe, i)
            for i in (B - 2, B - 1, B):
                tensor_body(pe, i)


def kernel(x, L0_tok_E0, L0_tok_E1, L0_tok_W0, L0_tok_b0, L0_tok_W1, L0_tok_b1, L0_tok_Wa, L0_tok_ba,
           L0_attn_Q, L0_attn_K, L0_attn_VO, L0_ffn_W1, L0_ffn_b1, L0_ffn_Wg, L0_ffn_bg, L0_ffn_Wd, L0_ffn_bd):
    import concourse.bacc as bacc
    from concourse.bass_utils import run_bass_kernel_spmd

    a = np.ascontiguousarray
    arrays = {
        "tokens": a(x),
        "emb": a(np.concatenate([np.asarray(L0_tok_E0), np.asarray(L0_tok_E1)], axis=1)),
        "W0": a(L0_tok_W0), "b0": a(np.asarray(L0_tok_b0).reshape(C, 1)),
        "W1": a(L0_tok_W1), "b1": a(np.asarray(L0_tok_b1).reshape(C, 1)),
        "Wa": a(np.asarray(L0_tok_Wa).reshape(1, C)), "ba": a(np.asarray(L0_tok_ba).reshape(1, 1)),
        "QT": a(np.asarray(L0_attn_Q).reshape(H * R, C).T), "KT": a(np.asarray(L0_attn_K).reshape(H * R, C).T),
        "VOT": a(np.asarray(L0_attn_VO).transpose(1, 0, 2).reshape(C, H * C)),
        "fW1": a(L0_ffn_W1), "fb1": a(np.asarray(L0_ffn_b1).reshape(M, P).T),
        "Wg": a(L0_ffn_Wg), "bg": a(np.asarray(L0_ffn_bg).reshape(1, NE)),
        "WdT": a(np.asarray(L0_ffn_Wd).transpose(1, 0, 2).reshape(HID, NE * C)),
        "bd": a(np.asarray(L0_ffn_bd).reshape(1, NE * C)),
    }
    nc = bacc.Bacc("TRN2", target_bir_lowering=False, num_devices=1)
    aps = {n: nc.dram_tensor(n, v.shape, mybir.dt.from_np(v.dtype), kind="ExternalInput").ap() for n, v in arrays.items()}
    out = nc.dram_tensor("out", (B, T, C), FP32, kind="ExternalOutput").ap()
    lm_tower(nc, out=out, **aps)
    r = run_bass_kernel_spmd(nc, [arrays], core_ids=[0])
    return r.results[0]["out"]
```

```python
from contextlib import ExitStack

import numpy as np

import concourse.bass as bass
from concourse import mybir

FP32 = mybir.dt.float32
FP32R = mybir.dt.float32r
INT32 = mybir.dt.int32
ALU = mybir.AluOpType
ACT = mybir.ActivationFunctionType
AX = mybir.AxisListType

B, T, C = 8, 512, 64
VOCAB, EMB = 25000, 75
H, R = 8, 32
HID, NE = 256, 8
P = 128
J = T // P
HG = P // R
G = H // HG
M = HID // P
NT = H * J
GT = HG * J
LEAD = NT - 8
Y_SLOTS = [23, 25, 28, 29]
S_BANKS, ST_BANKS, P_BUFS = 3, 2, 8
EPS = 1e-5
EXP_LN = "natural_log_exp_and_others"

SHARED = [("q0", 1), ("k0", 1), ("v0a", 1), ("v0b", 1), ("ctx_t", -1), ("q1", 1), ("k1", 1), ("x2_t", -1), ("row1", 0),
          ("hid0", -1), ("hid1", -1), ("v1a", 1), ("v1b", 1), ("e0_t", 2), ("e1_t", 2), ("gate", -1), ("proj", 2), ("y0", -1),
          ("proj_t", 2), ("y1", -1), ("y2", -1), ("row0", 1), ("y3", -1), ("x_t", 2)]
POS = {name: n for n, (name, _) in enumerate(SHARED)}
LINKS = {"alpha": 9, "ln1": 7, "ln2": 7, "h1": 1, "row": 4, "gate": 7}


def real(b):
    return not isinstance(b, int) or 0 <= b < B


def at_least(eng, sem, value):
    if not isinstance(value, int) or value > 0:
        eng.wait_ge(sem, value)


def lm_tower(nc, tokens, emb, W0, b0, W1, b1, Wa, ba, QT, KT, VOT, fW1, fb1, Wg, bg, WdT, bd, out):
    ctx = ExitStack()
    with ctx:
        def sb(name, shape, dt=FP32):
            return ctx.enter_context(nc.sbuf_tensor(name, shape, dt))

        def pb(name):
            return ctx.enter_context(nc.psum_tensor(name, [P, 512], FP32))

        def sem(name):
            return ctx.enter_context(nc.semaphore(name))

        ident = sb("ident", [P, P])
        emb_w = sb("emb_w", [EMB, 2, C])
        emb_b = sb("emb_b", [P, 1])
        wa = sb("wa", [P, C])
        ba_s = sb("ba_s", [P, 1])
        w_raw = sb("w_raw", [P, 256 + 256 + 512 + 256])
        w_hi = sb("w_hi", [P, 1280], FP32R)
        w_lo = sb("w_lo", [P, 1280], FP32R)
        QO, KO, VO_, FO = 0, 256, 512, 1024
        fb1_s = sb("fb1_s", [P, M])
        wg = sb("wg", [P, M, NE])
        bg_s = sb("bg_s", [P, NE])
        wd = sb("wd", [P, M, NE * C])
        bd_s = sb("bd_s", [P, NE * C])
        rank = sb("rank", [P, NE])
        half = sb("half", [P, J])

        idx = sb("idx", [P, J], INT32)
        rows = sb("rows", [P, J, 2 * EMB])
        rows_t = sb("rows_t", [EMB, 2, T])
        proj = sb("proj", [P, T])
        lw = sb("lw", [P, J * 2, C])
        logit = sb("logit", [P, J, 2])
        lmax = sb("lmax", [P, J])
        alpha = sb("alpha", [P, J, 2])
        lsum = sb("lsum", [P, J])
        h_now = sb("h_now", [P, J, C])
        h_all = sb("h_all", [P, B, J * C])
        mean = [sb(f"mean{n}", [P, J]) for n in range(2)]
        cent = [sb(f"cent{n}", [P, J, C]) for n in range(2)]
        sq = [sb(f"sq{n}", [P, J, C]) for n in range(2)]
        var = [sb(f"var{n}", [P, J]) for n in range(2)]
        rstd = [sb(f"rstd{n}", [P, J]) for n in range(2)]
        xs = [sb(f"xs{n}", [P, J, 2 * C], FP32R) for n in range(2)]
        xt = [sb(f"xt{n}", [P, T], FP32R) for n in range(2)]
        raw_q = [sb(f"raw_q{g}", [P, 2, T], FP32R) for g in range(G)]
        raw_k = [sb(f"raw_k{g}", [P, 2, T], FP32R) for g in range(G)]
        raw_v = [sb(f"raw_v{g}", [P, J, HG * C]) for g in range(G)]
        full_q = sb("full_q", [P, T])
        qst = sb("qst", [3 * R + 2, H, T], FP32R)
        kst = sb("kst", [3 * R + 2, H, T], FP32R)
        val = sb("val", [P, H, J, C])
        neg_max = sb("neg_max", [P, NT])
        den = sb("den", [P, NT])
        ln_den = sb("ln_den", [P, NT])
        shift = sb("shift", [P, J, HG])
        shift_s = sb("shift_s", [P, J, 2, HG], FP32R)
        shift_t = sb("shift_t", [2 * HG, T], FP32R)
        prob = sb("prob", [P, P_BUFS, T])
        ctx_s = sb("ctx_s", [P, T])
        h1 = sb("h1", [P, J, C])
        hid = sb("hid", [P, M, T])
        gl = sb("gl", [P, J, NE])
        gmax = sb("gmax", [P, J])
        gd = sb("gd", [P, J, NE])
        ge = sb("ge", [P, J, NE])
        gsum = sb("gsum", [P, J])
        gp = sb("gp", [P, J])
        geq = sb("geq", [P, J, NE])
        gtop = sb("gtop", [P, J])
        coef = sb("coef", [P, J, NE])
        yb = sb("yb", [P, 2, NE, C])
        yc = sb("yc", [P, NE, C])
        res = sb("res", [P, J, C])

        s_ps = [pb(f"s_ps{n}") for n in range(S_BANKS)]
        st_ps = [pb(f"st_ps{n}") for n in range(ST_BANKS)]
        ctx_ps = pb("ctx_ps")
        sh_ps = [pb(f"sh_ps{n}") for n in range(2)]

        def bank(name):
            return sh_ps[POS[name] % 2]

        w_loaded, w_split, const_ready = sem("w_loaded"), sem("w_split"), sem("const_ready")
        idx_loaded, rows_loaded, rows_free = sem("idx_loaded"), sem("rows_loaded"), sem("rows_free")
        filled = {name: sem(f"filled_{name}") for name, _ in SHARED}
        emptied = {name: sem(f"emptied_{name}") for name, _ in SHARED}
        alpha_in, alpha_exp = sem("alpha_in"), sem("alpha_exp")
        var_ready = [sem(f"var_ready{n}") for n in range(2)]
        rstd_ready = [sem(f"rstd_ready{n}") for n in range(2)]
        xs_ready = [sem(f"xs_ready{n}") for n in range(2)]
        stacked = [sem(f"stacked{h}") for h in range(H)]
        v_stored = [sem(f"v_stored{h}") for h in range(H)]
        s_done, max_done, s_exp = sem("s_done"), sem("max_done"), sem("s_exp")
        ln_done, shift_ready = sem("ln_done"), sem("shift_ready")
        shift_stored = [sem(f"shift_stored{g}") for g in range(G)]
        st_done, p_done, pv_done = sem("st_done"), sem("p_done"), sem("pv_done")
        ctx_read = sem("ctx_read")
        gate_in, gate_exp, coef_ready = sem("gate_in"), sem("gate_exp"), sem("coef_ready")
        y_used, res_ready, out_stored = sem("y_used"), sem("res_ready"), sem("out_stored")
        pool_step = sem("pool_step")
        pool_turn, sync_turn = sem("pool_turn"), sem("sync_turn")
        link_sem = {name: sem(f"link_{name}") for name in LINKS}
        STACK = 6 * 16

        block = ctx.enter_context(nc.Block())

        def s_tile(i, t):
            return (i, t + LEAD) if t < NT - LEAD else (i + 1, t + LEAD - NT)

        def lagged(i, t):
            return s_tile(i, t - 2) if t >= 2 else (i, LEAD - 2 + t)

        def wait_sync(sp, sema, value):
            at_least(sp, sema, value)
            if not isinstance(value, int):
                sp.sem_inc(sync_turn, 1)

        def load_idx(sp, b):
            wait_sync(sp, rows_loaded, 16 * J * b)
            sp.dma_start(idx[:, :], tokens[b, :].rearrange("(p j) -> p j", j=J)).then_inc(idx_loaded, 16)

        def stack_head(sp, b, h):
            g, r = h // HG, (h % HG) * R
            wait_sync(sp, emptied[f"q{g}"], b + 1)
            wait_sync(sp, emptied[f"k{g}"], b + 1)
            wait_sync(sp, st_done, NT * (b - 1) + J * (h + 1))
            for dst, src, parts in ((qst, raw_q, (0, 1, 0)), (kst, raw_k, (0, 0, 1))):
                for slot, part in enumerate(parts):
                    sp.dma_start(dst[slot * R:(slot + 1) * R, h, :].bitcast(FP32), src[g][r:r + R, part, :].bitcast(FP32)).then_inc(stacked[h], 16)

        def store_shift(sp, b, g):
            wait_sync(sp, emptied[f"row{g}"], b + 1)
            for part in range(2):
                sp.dma_start(qst[3 * R + part:3 * R + part + 1, g * HG:(g + 1) * HG, :].bitcast(FP32),
                             shift_t[part * HG:(part + 1) * HG, :].bitcast(FP32)).then_inc(shift_stored[g], 16)

        def store_out(sp, b):
            wait_sync(sp, res_ready, J * (b + 1))
            sp.dma_start(out[b, :, :].rearrange("(p j) c -> p (j c)", j=J), res[:, :, :].rearrange("p j c -> p (j c)")).then_inc(out_stored, 16)

        def sync_body(sp, i):
            for t in range(NT):
                if t == 0 and real(i + 2):
                    load_idx(sp, i + 2)
                if t % J == J - 1 and real(i + 1):
                    stack_head(sp, i + 1, t // J)
                if t == 12 and real(i):
                    store_shift(sp, i, 1)
                if t == 28 and real(i + 1):
                    store_shift(sp, i + 1, 0)
                if t == NT - 1 and real(i - 1):
                    store_out(sp, i - 1)

        @block.sync
        def _(sp):
            sp.sem_inc(out_stored, 16)
            for half_ in range(2):
                p = slice(half_ * C, (half_ + 1) * C)
                for off, src in ((QO, QT), (KO, KT), (VO_, VOT), (FO, fW1)):
                    sp.dma_start(w_raw[p, off:off + src.shape[1]], src).then_inc(w_loaded, 16)
            sp.dma_start(emb_w[:, 0, :], W0).then_inc(w_loaded, 16)
            sp.dma_start(emb_w[:, 1, :], W1).then_inc(w_loaded, 16)
            sp.dma_start(emb_b[0:C, :], b0).then_inc(w_loaded, 16)
            sp.dma_start(emb_b[C:P, :], b1).then_inc(w_loaded, 16)
            sp.dma_start(wa[:, :], Wa.to_broadcast([P, C])).then_inc(w_loaded, 16)
            sp.dma_start(ba_s[:, :], ba.to_broadcast([P, 1])).then_inc(w_loaded, 16)
            sp.dma_start(fb1_s[:, :], fb1).then_inc(w_loaded, 16)
            sp.dma_start(wg[:, :, :], Wg.rearrange("(m p) e -> p m e", p=P)).then_inc(w_loaded, 16)
            sp.dma_start(bg_s[:, :], bg.to_broadcast([P, NE])).then_inc(w_loaded, 16)
            sp.dma_start(wd[:, :, :], WdT.rearrange("(m p) f -> p m f", p=P)).then_inc(w_loaded, 16)
            sp.dma_start(bd_s[:, :], bd.to_broadcast([P, NE * C])).then_inc(w_loaded, 16)
            for i in (-2, -1, 0):
                sync_body(sp, i)
            with sp.Fori(1, B - 2) as i:
                sync_body(sp, i)
            for i in (B - 2, B - 1, B):
                sync_body(sp, i)
            sp.wait_ge(out_stored, 16 * (B + 1))

        W_ALL = 16 * (8 + 11)

        def gather(pool, b):
            at_least(pool, idx_loaded, 16 * (b + 1))
            at_least(pool, filled["e1_t"], b)
            pool.sem_inc(pool_turn, 1)
            for j in range(J):
                nc.gpsimd.indirect_dma_start(out=rows[:, j, :], out_offset=None, in_=emb,
                                             in_offset=bass.IndirectOffsetOnAxis(ap=idx[:, j:j + 1], axis=0)
                                             ).then_inc(rows_loaded, 16)

        def inverse_std(pool, b, n):
            at_least(pool, var_ready[n], b + 1)
            nc.gpsimd.tensor_tensor(rstd[n][:, :], var[n][:, :], half[:, :], ALU.pow).then_inc(rstd_ready[n], 1)

        def mix(pool, b, j):
            at_least(pool, emptied[f"y{j}"], b + 1)
            at_least(pool, coef_ready, b + 1)
            k = 4 * (J * b + j)
            if j:
                at_least(pool, res_ready, J * b + j)
            nc.gpsimd.tensor_tensor(yc[:, :, :], yb[:, j % 2, :, :], coef[:, j, :].unsqueeze(2).to_broadcast([P, NE, C]),
                                    ALU.mult).then_inc(pool_step, 1)
            pool.wait_ge(pool_step, k + 1)
            nc.gpsimd.tensor_tensor(yc[:, 0:4, :], yc[:, 0:4, :], yc[:, 4:8, :], ALU.add).then_inc(pool_step, 1)
            pool.wait_ge(pool_step, k + 2)
            nc.gpsimd.tensor_tensor(yc[:, 0:2, :], yc[:, 0:2, :], yc[:, 2:4, :], ALU.add).then_inc(pool_step, 1)
            pool.wait_ge(pool_step, k + 3)
            nc.gpsimd.tensor_tensor(yc[:, 0, :], yc[:, 0, :], yc[:, 1, :], ALU.add).then_inc(pool_step, 1)
            pool.wait_ge(pool_step, k + 4)
            nc.gpsimd.tensor_tensor(res[:, j, :], yc[:, 0, :], h1[:, j, :], ALU.add).then_inc(res_ready, 1)

        def store_v(pool, b, h):
            g = h // HG
            at_least(pool, emptied[f"v{g}a"], b + 1)
            at_least(pool, emptied[f"v{g}b"], b + 1)
            at_least(pool, pv_done, NT // 2 * (b - 1) + J // 2 * (h + 1))
            pool.sem_inc(pool_turn, 1)
            c0 = (h % HG) * C
            nc.gpsimd.tensor_copy(val[:, h, :, :], raw_v[g][:, :, c0:c0 + C]).then_inc(v_stored[h], 1)

        def pool_body(pool, i):
            for t in range(NT):
                if t == 3 and real(i):
                    store_v(pool, i, H - 1)
                if t == 8 and real(i - 1):
                    inverse_std(pool, i - 1, 1)
                if t == 9 and real(i + 2):
                    gather(pool, i + 2)
                if t % J == 3 and t >= 7 and real(i + 1):
                    store_v(pool, i + 1, t // J - 1)
                if t == 28 and real(i + 2):
                    inverse_std(pool, i + 2, 0)
                if t in Y_SLOTS and real(i - 1):
                    mix(pool, i - 1, Y_SLOTS.index(t))

        @block.gpsimd
        def _(pool):
            nc.gpsimd.memset(ident[:, :], 0.0).then_inc(const_ready, 1)
            pool.wait_ge(const_ready, 1)
            nc.gpsimd.affine_select(out=ident[:, :], in_=ident[:, :], compare_op=ALU.not_equal, fill=1.0, base=0,
                                    pattern=[[-1, P]], channel_multiplier=1).then_inc(const_ready, 1)
            nc.gpsimd.iota(rank[:, :], pattern=[[-1, NE]], base=NE, channel_multiplier=0,
                           allow_small_or_imprecise_dtypes=True).then_inc(const_ready, 1)
            nc.gpsimd.memset(half[:, :], -0.5).then_inc(const_ready, 1)
            pool.wait_ge(const_ready, 4)
            nc.gpsimd.memset(kst[3 * R:3 * R + 2, :, :].bitcast(FP32), 1.0).then_inc(const_ready, 1)
            pool.wait_ge(const_ready, 5)
            for i in (-2, -1, 0):
                pool_body(pool, i)
            with pool.Fori(1, B - 2) as i:
                pool_body(pool, i)
            for i in (B - 2, B - 1, B):
                pool_body(pool, i)

        def exp_scores(act, b, n):
            at_least(act, max_done, NT * b + n + 1)
            ps = s_ps[n % S_BANKS]
            nc.scalar.activation(ps[:, :], ps[:, :], ACT.Exp, bias=neg_max[:, n:n + 1], scale=-1.0,
                                 accum_out=den[:, n:n + 1]).then_inc(s_exp, 1)

        def exp_probs(act, b, n):
            at_least(act, st_done, NT * b + n + 1)
            at_least(act, pv_done, NT // 2 * b + n // 2 - P_BUFS // 2 + 1)
            nc.scalar.activation(prob[:, n % P_BUFS, :], st_ps[n % ST_BANKS][:, :], ACT.Exp, scale=-1.0).then_inc(p_done, 1)

        def log_sum(act, b, g):
            at_least(act, s_exp, NT * b + GT * (g + 1))
            nc.scalar.activation(ln_den[:, GT * g:GT * (g + 1)], den[:, GT * g:GT * (g + 1)], ACT.Ln).then_inc(ln_done, 1)

        def alpha_weights(act, b):
            at_least(act, alpha_in, b + 1)
            nc.scalar.activation(alpha[:, :, :], logit[:, :, :], ACT.Exp).then_inc(alpha_exp, 1)

        def gate_weights(act, b):
            at_least(act, gate_in, b + 1)
            nc.scalar.activation(ge[:, :, :], gd[:, :, :], ACT.Exp).then_inc(gate_exp, 1)

        def gelu(act, b, m):
            at_least(act, filled[f"hid{m}"], b + 1)
            nc.scalar.activation(hid[:, m, :], bank(f"hid{m}")[:, :], ACT.Gelu, bias=fb1_s[:, m:m + 1]).then_inc(emptied[f"hid{m}"], 1)

        def act_body(act, i):
            for t in range(NT):
                b, n = lagged(i, t)
                if real(b):
                    exp_scores(act, b, n)
                if real(i):
                    exp_probs(act, i, t)
                if t == 9 and real(i):
                    log_sum(act, i, 1)
                if t == 14 and real(i - 1):
                    for m in range(M):
                        gelu(act, i - 1, m)
                    act.preload_act_table_set(EXP_LN)
                if t == 22 and real(i - 1):
                    gate_weights(act, i - 1)
                if t == 25 and real(i + 2):
                    alpha_weights(act, i + 2)
                if t == 25 and real(i + 1):
                    log_sum(act, i + 1, 0)

        @block.scalar
        def _(act):
            act.preload_act_table_set(EXP_LN)
            act.wait_ge(w_loaded, W_ALL)
            for i in (-2, -1, 0):
                act_body(act, i)
            with act.Fori(1, B - 2) as i:
                act_body(act, i)
            for i in (B - 2, B - 1, B):
                act_body(act, i)

        def links(dve, name, b, before=0):
            count = [before]

            def link(ins):
                count[0] += 1
                ins.then_inc(link_sem[name], 1)
                dve.wait_ge(link_sem[name], LINKS[name] * b + count[0])
                assert count[0] <= LINKS[name]
            return link

        V = nc.vector

        def wide(small, n):
            return small.unsqueeze(2).to_broadcast([P, J, n])

        def row_max(dve, b, n):
            at_least(dve, s_done, NT * b + n + 1)
            V.tensor_reduce(neg_max[:, n:n + 1], s_ps[n % S_BANKS][:, :], AX.X, ALU.min).then_inc(max_done, 1)

        def rows_out(dve, b):
            for n in range(2):
                at_least(dve, filled[f"e{n}_t"], b + 1)
                V.tensor_copy(rows_t[:, n, :], bank(f"e{n}_t")[0:EMB, :]).then_inc(emptied[f"e{n}_t"], 1)

        def proj_out(dve, b):
            at_least(dve, filled["proj"], b + 1)
            V.tensor_scalar(proj[:, :], bank("proj")[:, :], emb_b[:, 0:1], None, ALU.add).then_inc(emptied["proj"], 1)

        def embedding_logits(dve, b):
            link = links(dve, "alpha", b)
            at_least(dve, filled["proj_t"], b + 1)
            ps = bank("proj_t")[:, :].rearrange("p (k c) -> p k c", c=C)
            lflat = logit[:, :, :].rearrange("p j n -> p (j n)")
            link(V.tensor_tensor(lw[:, :, :], ps, wa[:, :].unsqueeze(1).to_broadcast([P, 2 * J, C]), ALU.mult))
            link(V.tensor_reduce(lflat, lw[:, :, :], AX.X, ALU.add))
            link(V.tensor_scalar(lflat, lflat, ba_s[:, 0:1], None, ALU.add))
            link(V.tensor_reduce(lmax[:, :], logit[:, :, :], AX.X, ALU.max))
            V.tensor_tensor(logit[:, :, :], logit[:, :, :], wide(lmax[:, :], 2), ALU.subtract).then_inc(alpha_in, 1)

        def mix_embeddings(dve, b):
            link = links(dve, "alpha", b, 4)
            ps = bank("proj_t")[:, :].rearrange("p (k c) -> p k c", c=C)
            at_least(dve, alpha_exp, b + 1)
            link(V.tensor_reduce(lsum[:, :], alpha[:, :, :], AX.X, ALU.add))
            link(V.reciprocal(lsum[:, :], lsum[:, :]))
            link(V.tensor_tensor(alpha[:, :, :], alpha[:, :, :], wide(lsum[:, :], 2), ALU.mult))
            aflat = alpha[:, :, :].rearrange("p j n -> p (j n)").unsqueeze(2).to_broadcast([P, 2 * J, C])
            V.tensor_tensor(lw[:, :, :], ps, aflat, ALU.mult).then_inc(emptied["proj_t"], 1)
            at_least(dve, emptied["proj_t"], b + 1)
            w4 = lw[:, :, :].rearrange("p (j n) c -> p j n c", n=2)
            h_b = h_all[:, b, :].rearrange("p (j c) -> p j c", c=C)
            link(V.tensor_tensor(h_b, w4[:, :, 0, :], w4[:, :, 1, :], ALU.add))
            link(V.tensor_tensor(h_now[:, :, :], w4[:, :, 0, :], w4[:, :, 1, :], ALU.add))

        def centre(dve, b, n):
            x = (h_now, h1)[n][:, :, :]
            link = links(dve, f"ln{n + 1}", b)
            link(V.tensor_reduce(mean[n][:, :], x, AX.X, ALU.add))
            link(V.tensor_scalar(mean[n][:, :], mean[n][:, :], 1.0 / C, None, ALU.mult))
            link(V.tensor_tensor(cent[n][:, :, :], x, wide(mean[n][:, :], C), ALU.subtract))
            link(V.tensor_tensor(sq[n][:, :, :], cent[n][:, :, :], cent[n][:, :, :], ALU.mult))
            link(V.tensor_reduce(var[n][:, :], sq[n][:, :, :], AX.X, ALU.add))
            V.tensor_scalar(var[n][:, :], var[n][:, :], 1.0 / C, EPS, ALU.mult, ALU.add).then_inc(var_ready[n], 1)

        def normalise(dve, b, n):
            link = links(dve, f"ln{n + 1}", b, 5)
            at_least(dve, rstd_ready[n], b + 1)
            link(V.tensor_tensor(sq[n][:, :, :], cent[n][:, :, :], wide(rstd[n][:, :], C), ALU.mult))
            link(V.tensor_copy(xs[n][:, :, 0:C], sq[n][:, :, :]))
            V.tensor_tensor(xs[n][:, :, C:2 * C], sq[n][:, :, :], xs[n][:, :, 0:C].bitcast(FP32), ALU.subtract).then_inc(xs_ready[n], 1)

        def x_out(dve, b, n):
            name = ("x_t", "x2_t")[n]
            at_least(dve, filled[name], b + 1)
            V.tensor_copy(xt[n][:, :], bank(name)[:, :]).then_inc(emptied[name], 1)

        def split_qk(dve, b, g, which):
            name = f"{which}{g}"
            raw, scale = (raw_q, -1.0 / C ** 0.5) if which == "q" else (raw_k, 1.0)
            at_least(dve, filled[name], b + 1)
            if which == "q":
                for h in range(g * HG, (g + 1) * HG):
                    at_least(dve, stacked[h], STACK * b)
            ps = bank(name)[:, :]
            V.tensor_scalar(raw[g][:, 0, :], ps, scale, None, ALU.mult).then_inc(emptied[name + "_hi"], 1)
            dve.wait_ge(emptied[name + "_hi"], b + 1)
            V.scalar_tensor_tensor(raw[g][:, 1, :], ps, scale, raw[g][:, 0, :].bitcast(FP32), ALU.mult, ALU.subtract).then_inc(emptied[name], 1)

        for which in "qk":
            for g in range(G):
                emptied[f"{which}{g}_hi"] = sem(f"high_{which}{g}")

        def v_out(dve, b, g, part):
            name = f"v{g}" + "ab"[part]
            at_least(dve, filled[name], b + 1)
            if part == 0:
                for h in range(g * HG, (g + 1) * HG):
                    at_least(dve, v_stored[h], b)
            V.tensor_copy(raw_v[g][:, 2 * part:2 * part + 2, :].rearrange("p j c -> p (j c)"), bank(name)[:, :]).then_inc(emptied[name], 1)

        def shift_parts(dve, b, g):
            at_least(dve, ln_done, G * b + g + 1)
            cols = slice(GT * g, GT * (g + 1))
            ld = ln_den[:, cols].rearrange("p (h j) -> p j h", j=J)
            nm = neg_max[:, cols].rearrange("p (h j) -> p j h", j=J)
            V.tensor_tensor(shift[:, :, :], ld, nm, ALU.subtract).then_inc(link_sem["row"], 1)
            dve.wait_ge(link_sem["row"], 4 * b + 2 * g + 1)
            V.tensor_copy(shift_s[:, :, 0, :], shift[:, :, :]).then_inc(link_sem["row"], 1)
            dve.wait_ge(link_sem["row"], 4 * b + 2 * g + 2)
            V.tensor_tensor(shift_s[:, :, 1, :], shift[:, :, :], shift_s[:, :, 0, :].bitcast(FP32), ALU.subtract).then_inc(shift_ready, 1)

        def shift_out(dve, b, g):
            at_least(dve, filled[f"row{g}"], b + 1)
            if g == 0:
                at_least(dve, shift_stored[1], 32 * b)
            else:
                at_least(dve, shift_stored[0], 32 * (b + 1))
            V.tensor_copy(shift_t[:, :], bank(f"row{g}")[0:2 * HG, :]).then_inc(emptied[f"row{g}"], 1)

        def ctx_out(dve, b):
            at_least(dve, pv_done, NT // 2 * (b + 1))
            V.tensor_copy(ctx_s[:, :], ctx_ps[:, :]).then_inc(ctx_read, 1)

        def add_attention(dve, b):
            link = links(dve, "h1", b)
            at_least(dve, filled["ctx_t"], b + 1)
            ps = bank("ctx_t")[:, :].rearrange("p (j c) -> p j c", j=J)
            h_b = h_all[:, b, :].rearrange("p (j c) -> p j c", c=C)
            dve.wait_ge(out_stored, 16 * (b + 1))
            link(V.tensor_tensor(h1[:, :, :], ps[:, :, 0:C], h_b, ALU.add))
            V.tensor_tensor(h1[:, :, :], ps[:, :, C:2 * C], h1[:, :, :], ALU.add).then_inc(emptied["ctx_t"], 1)
            at_least(dve, emptied["ctx_t"], b + 1)

        def gate_logits(dve, b):
            link = links(dve, "gate", b)
            at_least(dve, filled["gate"], b + 1)
            ps = bank("gate")[:, 0:J * NE].rearrange("p (j e) -> p j e", e=NE)
            V.tensor_tensor(gl[:, :, :], ps, bg_s[:, :].unsqueeze(1).to_broadcast([P, J, NE]), ALU.add).then_inc(emptied["gate"], 1)
            at_least(dve, emptied["gate"], b + 1)
            link(V.tensor_reduce(gmax[:, :], gl[:, :, :], AX.X, ALU.max))
            V.tensor_tensor(gd[:, :, :], gl[:, :, :], wide(gmax[:, :], NE), ALU.subtract).then_inc(gate_in, 1)

        def route(dve, b):
            link = links(dve, "gate", b, 1)
            at_least(dve, gate_in, b + 1)
            link(V.tensor_scalar(geq[:, :, :], gd[:, :, :], 0.0, None, ALU.is_ge))
            link(V.tensor_tensor(geq[:, :, :], geq[:, :, :], rank[:, :].unsqueeze(1).to_broadcast([P, J, NE]), ALU.mult))
            link(V.tensor_reduce(gtop[:, :], geq[:, :, :], AX.X, ALU.max))
            link(V.tensor_tensor(geq[:, :, :], geq[:, :, :], wide(gtop[:, :], NE), ALU.is_equal))
            at_least(dve, gate_exp, b + 1)
            link(V.tensor_reduce(gsum[:, :], ge[:, :, :], AX.X, ALU.add))
            link(V.reciprocal(gp[:, :], gsum[:, :]))
            V.tensor_tensor(coef[:, :, :], geq[:, :, :], wide(gp[:, :], NE), ALU.mult).then_inc(coef_ready, 1)

        def y_out(dve, b, j):
            at_least(dve, filled[f"y{j}"], b + 1)
            if j >= 2:
                at_least(dve, res_ready, J * b + j - 1)
            V.tensor_tensor(yb[:, j % 2, :, :].rearrange("p e c -> p (e c)"), bank(f"y{j}")[:, :], bd_s[:, :], ALU.add).then_inc(emptied[f"y{j}"], 1)

        def vector_body(dve, i):
            for t in range(NT):
                b, n = s_tile(i, t)
                if real(b):
                    row_max(dve, b, n)
                if real(i - 1):
                    if t == 3:
                        ctx_out(dve, i - 1)
                    if t == 6:
                        add_attention(dve, i - 1)
                    if t == 7:
                        centre(dve, i - 1, 1)
                    if t == 9:
                        normalise(dve, i - 1, 1)
                    if t == 11:
                        x_out(dve, i - 1, 1)
                    if t == 21:
                        gate_logits(dve, i - 1)
                    if t == 23:
                        route(dve, i - 1)
                    if t in Y_SLOTS:
                        y_out(dve, i - 1, Y_SLOTS.index(t))
                if real(i):
                    if t == 10:
                        shift_parts(dve, i, 1)
                    if t == 12:
                        shift_out(dve, i, 1)
                if real(i + 1):
                    if t == 0:
                        x_out(dve, i + 1, 0)
                    if t == 2:
                        split_qk(dve, i + 1, 0, "q")
                    if t == 3:
                        split_qk(dve, i + 1, 0, "k")
                    if t in (4, 5):
                        v_out(dve, i + 1, 0, t - 4)
                    if t == 9:
                        split_qk(dve, i + 1, 1, "q")
                    if t == 10:
                        split_qk(dve, i + 1, 1, "k")
                    if t in (17, 18):
                        v_out(dve, i + 1, 1, t - 17)
                    if t == 26:
                        shift_parts(dve, i + 1, 0)
                    if t == 28:
                        shift_out(dve, i + 1, 0)
                if real(i + 2):
                    if t == 19:
                        rows_out(dve, i + 2)
                    if t == 22:
                        proj_out(dve, i + 2)
                    if t == 24:
                        embedding_logits(dve, i + 2)
                    if t == 26:
                        mix_embeddings(dve, i + 2)
                    if t == 27:
                        centre(dve, i + 2, 0)
                    if t == 30:
                        normalise(dve, i + 2, 0)

        @block.vector
        def _(dve):
            dve.wait_ge(w_loaded, W_ALL)
            V.tensor_copy(w_hi[:, :], w_raw[:, :]).then_inc(w_split, 1)
            dve.wait_ge(w_split, 1)
            V.tensor_tensor(w_lo[:, :], w_raw[:, :], w_hi[:, :].bitcast(FP32), ALU.subtract).then_inc(w_split, 1)
            dve.wait_ge(const_ready, 5)
            for i in (-2, -1, 0):
                vector_body(dve, i)
            with dve.Fori(1, B - 2) as i:
                vector_body(dve, i)
            for i in (B - 2, B - 1, B):
                vector_body(dve, i)

        PE = nc.tensor

        def claim(pe, i, name):
            at = POS[name] - 2
            body = i
            for _ in range(3 * len(SHARED)):
                if at < 0:
                    at += len(SHARED)
                    body = body - 1
                prev, rel = SHARED[at]
                if isinstance(body + rel, int) and body + rel < 0 and body < -3:
                    return
                if real(body + rel):
                    at_least(pe, emptied[prev], body + rel + 1)
                    return
                at -= 2

        def scores(pe, b, n):
            h, c = divmod(n, J)
            if c == 0:
                pe.wait_ge(stacked[h], STACK * (b + 1))
            if n < S_BANKS:
                last = max(m for m in range(NT) if m % S_BANKS == n)
                at_least(pe, s_exp, NT * (b - 1) + last + 1)
            else:
                at_least(pe, s_exp, NT * b + n - S_BANKS + 1)
            PE.matmul(s_ps[n % S_BANKS][:, :], qst[0:3 * R, h, c * P:(c + 1) * P], kst[0:3 * R, h, :],
                      start=True, stop=True).then_inc(s_done, 1)

        def scores_t(pe, b, n):
            h, c = divmod(n, J)
            if n % GT == 0:
                pe.wait_ge(shift_stored[n // GT], 32 * (b + 1))
            at_least(pe, p_done, NT * b + n - ST_BANKS + 1)
            PE.matmul(st_ps[n % ST_BANKS][:, :], kst[:, h, c * P:(c + 1) * P], qst[:, h, :],
                      start=True, stop=True).then_inc(st_done, 1)

        def context(pe, b, pair):
            h, c = divmod(2 * pair, J)
            if c == 0:
                pe.wait_ge(v_stored[h], b + 1)
            if pair == 0:
                at_least(pe, ctx_read, b)
            pe.wait_ge(p_done, NT * b + 2 * pair + 2)
            for d in range(2):
                last = PE.matmul(ctx_ps[d * C:(d + 1) * C, :], val[:, h, c + d, :], prob[:, (2 * pair + d) % P_BUFS, :],
                                 start=(pair == 0), stop=(pair == NT // 2 - 1))
            last.then_inc(pv_done, 1)

        def transposes(pe, i, name, pieces, rows_):
            claim(pe, i, name)
            for j, piece in enumerate(pieces):
                last = PE.transpose(bank(name)[0:rows_, j * P:(j + 1) * P], piece, ident[:, :])
            last.then_inc(filled[name], 1)

        def embed_t(pe, i, b):
            at_least(pe, rows_loaded, 16 * J * (b + 1))
            for n in range(2):
                transposes(pe, i, f"e{n}_t", [rows[:, j, n * EMB:(n + 1) * EMB] for j in range(J)], EMB)

        def embed_proj(pe, i, b):
            claim(pe, i, "proj")
            for n in range(2):
                at_least(pe, emptied[f"e{n}_t"], b + 1)
                last = PE.matmul(bank("proj")[n * C:(n + 1) * C, :], emb_w[:, n, :], rows_t[:, n, :], start=True, stop=True)
            last.then_inc(filled["proj"], 1)

        def two_pass(out_ap, parts, moving, off=None):
            PE.matmul(out_ap, parts[0], moving, start=True, stop=False)
            return PE.matmul(out_ap, parts[1], moving, start=False, stop=True)

        def project_qk(pe, i, b, g, which):
            name = f"{which}{g}"
            claim(pe, i, name)
            at_least(pe, emptied["x_t"], b + 1)
            o = (QO if which == "q" else KO) + g * P
            two_pass(bank(name)[:, :], (w_hi[:, o:o + P], w_lo[:, o:o + P]), xt[0][:, :]).then_inc(filled[name], 1)

        def project_v(pe, i, b, g, part):
            name = f"v{g}" + "ab"[part]
            claim(pe, i, name)
            at_least(pe, emptied["x_t"], b + 1)
            o = VO_ + g * HG * C
            for d in range(2):
                tok = slice((2 * part + d) * P, (2 * part + d + 1) * P)
                dst = bank(name)[:, d * HG * C:(d + 1) * HG * C]
                PE.matmul(dst, xt[0][:, tok], w_hi[:, o:o + HG * C], start=True, stop=False)
                last = PE.matmul(dst, xt[0][:, tok], w_lo[:, o:o + HG * C], start=False, stop=True)
            last.then_inc(filled[name], 1)

        def shift_row(pe, i, b, g):
            at_least(pe, shift_ready, G * b + g + 1)
            transposes(pe, i, f"row{g}", [shift_s[:, j, :, :].bitcast(FP32).rearrange("p a h -> p (a h)") for j in range(J)], 2 * HG)

        def hidden(pe, i, b, m):
            name = f"hid{m}"
            claim(pe, i, name)
            at_least(pe, emptied["x2_t"], b + 1)
            o = FO + m * P
            two_pass(bank(name)[:, :], (w_hi[:, o:o + P], w_lo[:, o:o + P]), xt[1][:, :]).then_inc(filled[name], 1)

        def gate(pe, i, b):
            claim(pe, i, "gate")
            for m in range(M):
                at_least(pe, emptied[f"hid{m}"], b + 1)
            for j in range(J):
                for m in range(M):
                    last = PE.matmul(bank("gate")[:, j * NE:(j + 1) * NE], hid[:, m, j * P:(j + 1) * P], wg[:, m, :],
                                     start=(m == 0), stop=(m == M - 1))
            last.then_inc(filled["gate"], 1)

        def experts(pe, i, b, j):
            name = f"y{j}"
            claim(pe, i, name)
            for m in range(M):
                last = PE.matmul(bank(name)[:, :], hid[:, m, j * P:(j + 1) * P], wd[:, m, :], start=(m == 0), stop=(m == M - 1))
            last.then_inc(filled[name], 1)

        def tensor_body(pe, i):
            for t in range(NT):
                b, n = s_tile(i, t)
                if real(b):
                    scores(pe, b, n)
                if real(i):
                    scores_t(pe, i, t)
                if t in (0, 2) and real(i - 1):
                    context(pe, i - 1, NT // 2 - 2 + t // 2)
                if t % 2 == 0 and t >= 4 and real(i):
                    context(pe, i, t // 2 - 2)
                if real(i - 1):
                    if t == 5:
                        at_least(pe, ctx_read, i)
                        transposes(pe, i, "ctx_t", [ctx_s[:, j * P:(j + 1) * P] for j in range(J)], P)
                    if t == 10:
                        at_least(pe, xs_ready[1], i)
                        transposes(pe, i, "x2_t", [xs[1][:, j, :].bitcast(FP32) for j in range(J)], P)
                    if t in (12, 13):
                        hidden(pe, i, i - 1, t - 12)
                    if t == 20:
                        gate(pe, i, i - 1)
                if t == 11 and real(i):
                    shift_row(pe, i, i, 1)
                if real(i + 1):
                    if t == 1:
                        project_qk(pe, i, i + 1, 0, "q")
                    if t == 2:
                        project_qk(pe, i, i + 1, 0, "k")
                    if t in (3, 4):
                        project_v(pe, i, i + 1, 0, t - 3)
                    if t == 8:
                        project_qk(pe, i, i + 1, 1, "q")
                    if t == 9:
                        project_qk(pe, i, i + 1, 1, "k")
                    if t in (16, 17):
                        project_v(pe, i, i + 1, 1, t - 16)
                if real(i + 2):
                    if t == 18:
                        embed_t(pe, i, i + 2)
                    if t == 21:
                        embed_proj(pe, i, i + 2)
                    if t == 23:
                        at_least(pe, emptied["proj"], i + 3)
                        transposes(pe, i, "proj_t", [proj[:, j * P:(j + 1) * P] for j in range(J)], P)
                if t + 1 in Y_SLOTS and real(i - 1):
                    experts(pe, i, i - 1, Y_SLOTS.index(t + 1))
                if t == 27 and real(i + 1):
                    shift_row(pe, i, i + 1, 0)
                if t == 31 and real(i + 2):
                    at_least(pe, xs_ready[0], i + 3)
                    transposes(pe, i, "x_t", [xs[0][:, j, :].bitcast(FP32) for j in range(J)], P)

        @block.tensor
        def _(pe):
            pe.wait_ge(const_ready, 5)
            pe.wait_ge(w_split, 2)
            for i in (-2, -1, 0):
                tensor_body(pe, i)
            with pe.Fori(1, B - 2) as i:
                tensor_body(pe, i)
            for i in (B - 2, B - 1, B):
                tensor_body(pe, i)


def kernel(x, L0_tok_E0, L0_tok_E1, L0_tok_W0, L0_tok_b0, L0_tok_W1, L0_tok_b1, L0_tok_Wa, L0_tok_ba,
           L0_attn_Q, L0_attn_K, L0_attn_VO, L0_ffn_W1, L0_ffn_b1, L0_ffn_Wg, L0_ffn_bg, L0_ffn_Wd, L0_ffn_bd):
    import concourse.bacc as bacc
    from concourse.bass_utils import run_bass_kernel_spmd

    a = np.ascontiguousarray
    arrays = {
        "tokens": a(x),
        "emb": a(np.concatenate([np.asarray(L0_tok_E0), np.asarray(L0_tok_E1)], axis=1)),
        "W0": a(L0_tok_W0), "b0": a(np.asarray(L0_tok_b0).reshape(C, 1)),
        "W1": a(L0_tok_W1), "b1": a(np.asarray(L0_tok_b1).reshape(C, 1)),
        "Wa": a(np.asarray(L0_tok_Wa).reshape(1, C)), "ba": a(np.asarray(L0_tok_ba).reshape(1, 1)),
        "QT": a(np.asarray(L0_attn_Q).reshape(H * R, C).T), "KT": a(np.asarray(L0_attn_K).reshape(H * R, C).T),
        "VOT": a(np.asarray(L0_attn_VO).transpose(1, 0, 2).reshape(C, H * C)),
        "fW1": a(L0_ffn_W1), "fb1": a(np.asarray(L0_ffn_b1).reshape(M, P).T),
        "Wg": a(L0_ffn_Wg), "bg": a(np.asarray(L0_ffn_bg).reshape(1, NE)),
        "WdT": a(np.asarray(L0_ffn_Wd).transpose(1, 0, 2).reshape(HID, NE * C)),
        "bd": a(np.asarray(L0_ffn_bd).reshape(1, NE * C)),
    }
    nc = bacc.Bacc("TRN2", target_bir_lowering=False, num_devices=1)
    aps = {n: nc.dram_tensor(n, v.shape, mybir.dt.from_np(v.dtype), kind="ExternalInput").ap() for n, v in arrays.items()}
    out = nc.dram_tensor("out", (B, T, C), FP32, kind="ExternalOutput").ap()
    lm_tower(nc, out=out, **aps)
    r = run_bass_kernel_spmd(nc, [arrays], core_ids=[0])
    return r.results[0]["out"]
```

```python
from contextlib import ExitStack

import numpy as np

import concourse.bass as bass
from concourse import mybir

FP32 = mybir.dt.float32
FP32R = mybir.dt.float32r
INT32 = mybir.dt.int32
ALU = mybir.AluOpType
ACT = mybir.ActivationFunctionType
AX = mybir.AxisListType

B, T, C = 8, 512, 64
EMB = 75
H, R = 8, 32
HID, NE = 256, 8
P = 128
J = T // P
HG = P // R
G = H // HG
M = HID // P
NT = H * J
GT = HG * J
LEAD = NT - 8
S_BANKS, ST_BANKS, SH_BANKS = 3, 2, 2
P_BUFS = 8
LAG_S = 2
LAG_PV = 4
EPS = 1e-5
EXP_LN = "natural_log_exp_and_others"

WHEN_T = {
    "ctx_t": 100, "x2_t": 107, "row0": 60, "row1": 77, "hid0": 108, "hid1": 108, "gate": 110, "q0": 34,
    "k0": 34, "v0a": 37, "v0b": 38, "q1": 39, "k1": 47, "v1a": 39, "v1b": 45, "e0_t": 8, "e1_t": 13,
    "proj": 18, "proj_t": 20, "y0": 118, "y1": 120, "y2": 122, "y3": 126, "x_t": 31}
WHEN_V = {
    "hid0": 107, "hid1": 108, "ctx": 98, "h1": 100, "layer0": 25, "layer1": 101, "normal0": 29,
    "normal1": 104, "x_t": 31, "x2_t": 106, "gate": 113, "tops": 113, "route": 120, "y0": 119, "y1": 120,
    "y2": 123, "y3": 126, "parts0": 58, "row0": 59, "parts1": 75, "row1": 76, "q0": 34, "k0": 34, "v0a": 36,
    "v0b": 38, "q1": 38, "k1": 47, "v1a": 41, "v1b": 45, "e0_t": 10, "e1_t": 14, "proj": 18, "logits": 20,
    "alpha": 22}
WHEN_A = {
    "ln1": 76, "gelu": 109, "gate": 118, "alpha": 22, "ln0": 58}
WHEN_G = {
    "power1": 104, "gather": 0, "power0": 26, "mix0": 121, "mix1": 121, "mix2": 125, "mix3": 127, "v": 40}
WHEN_S = {
    "idx": 1, "stack": 33, "shift1": 76, "shift0": 57, "out": 126}
SHARED = [(name, 2 - when // NT) for name, when in sorted(WHEN_T.items(), key=lambda item: item[1] % NT)]
POS = {name: n for n, (name, _) in enumerate(SHARED)}
LINKS = {"alpha": 9, "ln1": 7, "ln2": 7, "h1": 1, "row": 4, "gate": 7}


def real(b):
    return not isinstance(b, int) or 0 <= b < B


def due(i, t, when):
    k, slot = divmod(when, NT)
    b = i if k == 2 else i + (2 - k)
    return [b] if slot == t and real(b) else []


def at_least(eng, sem, value):
    if not isinstance(value, int) or value > 0:
        eng.wait_ge(sem, value)


def lm_tower(nc, tokens, emb, emb_W, emb_B, wa_ba, weights, fb1, Wg, bg_bd, WdT, out):
    ctx = ExitStack()
    with ctx:
        def sb(name, shape, dt=FP32):
            return ctx.enter_context(nc.sbuf_tensor(name, shape, dt))

        def pb(name):
            return ctx.enter_context(nc.psum_tensor(name, [P, 512], FP32))

        def sem(name):
            return ctx.enter_context(nc.semaphore(name))

        ident = sb("ident", [P, P])
        emb_w = sb("emb_w", [EMB, 2, C])
        emb_b = sb("emb_b", [P, 1])
        wa = sb("wa", [P, C + 1])
        w_raw = sb("w_raw", [P, 256 + 256 + 512 + 256])
        w_hi = sb("w_hi", [P, 1280], FP32R)
        w_lo = sb("w_lo", [P, 1280], FP32R)
        QO, KO, VO_, FO = 0, 256, 512, 1024
        fb1_s = sb("fb1_s", [P, M])
        wg = sb("wg", [P, M, NE])
        bg_bd_s = sb("bg_bd_s", [P, NE + NE * C])
        wd = sb("wd", [P, M, NE * C])
        rank = sb("rank", [P, NE])
        half = sb("half", [P, J])

        idx = sb("idx", [P, J], INT32)
        rows = sb("rows", [P, J, 2 * EMB])
        rows_t = sb("rows_t", [EMB, 2, T])
        proj = sb("proj", [P, T])
        lw = sb("lw", [P, J * 2, C])
        logit = sb("logit", [P, J, 2])
        lmax = sb("lmax", [P, J])
        alpha = sb("alpha", [P, J, 2])
        lsum = sb("lsum", [P, J])
        h_now = sb("h_now", [P, J, C])
        h_all = sb("h_all", [P, B, J * C])
        mean = [sb(f"mean{n}", [P, J]) for n in range(2)]
        cent = [sb(f"cent{n}", [P, J, C]) for n in range(2)]
        sq = [sb(f"sq{n}", [P, J, C]) for n in range(2)]
        var = [sb(f"var{n}", [P, J]) for n in range(2)]
        rstd = [sb(f"rstd{n}", [P, J]) for n in range(2)]
        xs = [sb(f"xs{n}", [P, J, 2 * C], FP32R) for n in range(2)]
        xt = [sb(f"xt{n}", [P, T], FP32R) for n in range(2)]
        raw_q = [sb(f"raw_q{g}", [P, 2, T], FP32R) for g in range(G)]
        raw_k = [sb(f"raw_k{g}", [P, 2, T], FP32R) for g in range(G)]
        raw_v = [sb(f"raw_v{g}", [P, J, HG * C]) for g in range(G)]
        full_q = sb("full_q", [P, T])
        qst = sb("qst", [3 * R + 2, H, T], FP32R)
        kst = sb("kst", [3 * R + 2, H, T], FP32R)
        val = sb("val", [P, H, J, C])
        neg_max = sb("neg_max", [P, NT])
        den = sb("den", [P, NT])
        ln_den = sb("ln_den", [P, NT])
        shift = sb("shift", [P, J, HG])
        shift_s = sb("shift_s", [P, J, 2, HG], FP32R)
        shift_t = sb("shift_t", [2 * HG, T], FP32R)
        prob = sb("prob", [P, P_BUFS, T])
        ctx_s = sb("ctx_s", [P, T])
        h1 = sb("h1", [P, J, C])
        hid = sb("hid", [P, M, T])
        gl = sb("gl", [P, J, NE])
        gmax = sb("gmax", [P, J])
        gd = sb("gd", [P, J, NE])
        ge = sb("ge", [P, J, NE])
        gsum = sb("gsum", [P, J])
        gp = sb("gp", [P, J])
        geq = sb("geq", [P, J, NE])
        gtop = sb("gtop", [P, J])
        coef = sb("coef", [P, J, NE])
        yb = sb("yb", [P, 2, NE, C])
        yc = sb("yc", [P, NE, C])
        res = sb("res", [P, J, C])

        s_ps = [pb(f"s_ps{n}") for n in range(S_BANKS)]
        st_ps = [pb(f"st_ps{n}") for n in range(ST_BANKS)]
        ctx_ps = pb("ctx_ps")
        sh_ps = [pb(f"sh_ps{n}") for n in range(SH_BANKS)]

        def bank(name):
            return sh_ps[POS[name] % SH_BANKS]

        emb_loaded, w_loaded, late_loaded = sem("emb_loaded"), sem("w_loaded"), sem("late_loaded")
        w_split, ident_ready, const_ready, ones_ready = sem("w_split"), sem("ident_ready"), sem("const_ready"), sem("ones_ready")
        idx_loaded, rows_loaded = sem("idx_loaded"), sem("rows_loaded")
        filled = {name: sem(f"filled_{name}") for name, _ in SHARED}
        emptied = {name: sem(f"emptied_{name}") for name, _ in SHARED}
        high_ready = {f"{w}{g}": sem(f"high_ready_{w}{g}") for w in "qk" for g in range(G)}
        alpha_in, alpha_exp = sem("alpha_in"), sem("alpha_exp")
        var_ready = [sem(f"var_ready{n}") for n in range(2)]
        rstd_ready = [sem(f"rstd_ready{n}") for n in range(2)]
        xs_ready = [sem(f"xs_ready{n}") for n in range(2)]
        stacked = [sem(f"stacked{h}") for h in range(H)]
        v_stored = [sem(f"v_stored{h}") for h in range(H)]
        s_done, max_done, s_exp = sem("s_done"), sem("max_done"), sem("s_exp")
        ln_done, shift_ready = sem("ln_done"), sem("shift_ready")
        shift_stored = [sem(f"shift_stored{g}") for g in range(G)]
        st_done, p_done, pv_done = sem("st_done"), sem("p_done"), sem("pv_done")
        ctx_read = sem("ctx_read")
        gate_in, gate_exp, coef_ready = sem("gate_in"), sem("gate_exp"), sem("coef_ready")
        hid_ready = sem("hid_ready")
        res_ready, out_stored = sem("res_ready"), sem("out_stored")
        pool_step, tail_step, tail_mixed = sem("pool_step"), sem("tail_step"), sem("tail_mixed")
        pool_turn, sync_turn = sem("pool_turn"), sem("sync_turn")
        link_sem = {name: sem(f"link_{name}") for name in LINKS}
        STACK = 6 * 16

        block = ctx.enter_context(nc.Block())

        def s_tile(i, t):
            return (i, t + LEAD) if t < NT - LEAD else (i + 1, t + LEAD - NT)

        def lagged(i, t):
            return s_tile(i, t - LAG_S) if t >= LAG_S else (i, LEAD - LAG_S + t)

        def wait_sync(sp, sema, value):
            at_least(sp, sema, value)
            if not isinstance(value, int):
                sp.sem_inc(sync_turn, 1)

        def load_idx(sp, b):
            wait_sync(sp, rows_loaded, 16 * J * b)
            sp.dma_start(idx[:, :], tokens[b, :].rearrange("(p j) -> p j", j=J)).then_inc(idx_loaded, 16)

        def stack_head(sp, b, h):
            g, r = h // HG, (h % HG) * R
            wait_sync(sp, emptied[f"q{g}"], b + 2)
            wait_sync(sp, emptied[f"k{g}"], b + 2)
            wait_sync(sp, st_done, NT * (b - 1) + J * (h + 1))
            for dst, src, parts in ((qst, raw_q, (0, 1, 0)), (kst, raw_k, (0, 0, 1))):
                for slot, part in enumerate(parts):
                    sp.dma_start(dst[slot * R:(slot + 1) * R, h, :].bitcast(FP32), src[g][r:r + R, part, :].bitcast(FP32)).then_inc(stacked[h], 16)

        def store_shift(sp, b, g):
            wait_sync(sp, emptied[f"row{g}"], b + 2)
            for part in range(2):
                sp.dma_start(qst[3 * R + part:3 * R + part + 1, g * HG:(g + 1) * HG, :].bitcast(FP32),
                             shift_t[part * HG:(part + 1) * HG, :].bitcast(FP32)).then_inc(shift_stored[g], 16)

        def store_out(sp, b):
            if isinstance(b, int) and b == B - 1:
                sp.wait_ge(res_ready, J * (b + 1) + J // 2)
                sp.wait_ge(tail_mixed, J // 2)
            else:
                wait_sync(sp, res_ready, J * (b + 2))
            sp.dma_start(out[b, :, :].rearrange("(p j) c -> p (j c)", j=J), res[:, :, :].rearrange("p j c -> p (j c)")).then_inc(out_stored, 16)

        def sync_body(sp, i):
            for t in range(NT):
                for b in due(i, t, WHEN_S["idx"]):
                    if not isinstance(b, int) or b > 0:
                        load_idx(sp, b)
                for h in range(H):
                    for b in due(i, t, WHEN_S["stack"] + J * h):
                        stack_head(sp, b, h)
                for b in due(i, t, WHEN_S["shift1"]):
                    store_shift(sp, b, 1)
                for b in due(i, t, WHEN_S["shift0"]):
                    store_shift(sp, b, 0)
                for b in due(i, t, WHEN_S["out"]):
                    store_out(sp, b)

        @block.sync
        def _(sp):
            load_idx(sp, 0)
            sp.dma_start(emb_w[:, :, :], emb_W).then_inc(emb_loaded, 16)
            sp.dma_start(emb_b[:, :], emb_B).then_inc(emb_loaded, 16)
            sp.dma_start(wa[:, :], wa_ba.to_broadcast([P, C + 1])).then_inc(emb_loaded, 16)
            for half_ in range(2):
                sp.dma_start(w_raw[half_ * C:(half_ + 1) * C, :], weights).then_inc(w_loaded, 16)
            sp.dma_start(fb1_s[:, :], fb1).then_inc(late_loaded, 16)
            sp.dma_start(wg[:, :, :], Wg.rearrange("(m p) e -> p m e", p=P)).then_inc(late_loaded, 16)
            sp.dma_start(bg_bd_s[:, :], bg_bd.to_broadcast([P, NE + NE * C])).then_inc(late_loaded, 16)
            sp.dma_start(wd[:, :, :], WdT.rearrange("(m p) f -> p m f", p=P)).then_inc(late_loaded, 16)
            sp.sem_inc(out_stored, 16)
            sp.sem_inc(res_ready, J)
            for name, _ in SHARED:
                sp.sem_inc(emptied[name], 1)
            for i in (-2, -1, 0):
                sync_body(sp, i)
            with sp.Fori(1, B - 2) as i:
                sync_body(sp, i)
            for i in (B - 2, B - 1, B):
                sync_body(sp, i)
            sp.wait_ge(out_stored, 16 * (B + 1))

        EMB_ALL, W_ALL, LATE_ALL = 16 * 3, 16 * 2, 16 * 4

        def gather(pool, b):
            at_least(pool, idx_loaded, 16 * (b + 1))
            at_least(pool, filled["e1_t"], b)
            pool.sem_inc(pool_turn, 1)
            for j in range(J):
                nc.gpsimd.indirect_dma_start(out=rows[:, j, :], out_offset=None, in_=emb,
                                             in_offset=bass.IndirectOffsetOnAxis(ap=idx[:, j:j + 1], axis=0)
                                             ).then_inc(rows_loaded, 16)

        def inverse_std(pool, b, n):
            at_least(pool, var_ready[n], b + 1)
            nc.gpsimd.tensor_tensor(rstd[n][:, :], var[n][:, :], half[:, :], ALU.pow).then_inc(rstd_ready[n], 1)

        def mix(pool, b, j):
            last = isinstance(b, int) and b == B - 1
            if last and j % 2:
                return
            at_least(pool, emptied[f"y{j}"], b + 2)
            at_least(pool, coef_ready, b + 1)
            k = 4 * (J * b + j)
            if last:
                k, j_before = 4 * (J * b + j // 2), j // 2
            else:
                j_before = j
            if j == 0:
                pool.wait_ge(out_stored, 16 * (b + 1))
            else:
                at_least(pool, res_ready, J * (b + 1) + j_before)
            nc.gpsimd.tensor_tensor(yc[:, :, :], yb[:, j % 2, :, :], coef[:, j, :].unsqueeze(2).to_broadcast([P, NE, C]),
                                    ALU.mult).then_inc(pool_step, 1)
            pool.wait_ge(pool_step, k + 1)
            nc.gpsimd.tensor_tensor(yc[:, 0:4, :], yc[:, 0:4, :], yc[:, 4:8, :], ALU.add).then_inc(pool_step, 1)
            pool.wait_ge(pool_step, k + 2)
            nc.gpsimd.tensor_tensor(yc[:, 0:2, :], yc[:, 0:2, :], yc[:, 2:4, :], ALU.add).then_inc(pool_step, 1)
            pool.wait_ge(pool_step, k + 3)
            nc.gpsimd.tensor_tensor(yc[:, 0, :], yc[:, 0, :], yc[:, 1, :], ALU.add).then_inc(pool_step, 1)
            pool.wait_ge(pool_step, k + 4)
            nc.gpsimd.tensor_tensor(res[:, j, :], yc[:, 0, :], h1[:, j, :], ALU.add).then_inc(res_ready, 1)

        def store_v(pool, b, h):
            g = h // HG
            at_least(pool, emptied[f"v{g}a"], b + 2)
            at_least(pool, emptied[f"v{g}b"], b + 2)
            at_least(pool, pv_done, NT // 2 * (b - 1) + J // 2 * (h + 1))
            pool.sem_inc(pool_turn, 1)
            c0 = (h % HG) * C
            nc.gpsimd.tensor_copy(val[:, h, :, :], raw_v[g][:, :, c0:c0 + C]).then_inc(v_stored[h], 1)

        def pool_body(pool, i):
            for t in range(NT):
                for b in due(i, t, WHEN_G["power1"]):
                    inverse_std(pool, b, 1)
                for b in due(i, t, WHEN_G["power0"]):
                    inverse_std(pool, b, 0)
                for h in range(H):
                    for b in due(i, t, WHEN_G["v"] + J * h):
                        store_v(pool, b, h)
                for b in due(i, t, WHEN_G["gather"]):
                    gather(pool, b)
                for j in range(J):
                    for b in due(i, t, WHEN_G[f"mix{j}"]):
                        mix(pool, b, j)

        @block.gpsimd
        def _(pool):
            nc.gpsimd.memset(ident[:, :], 0.0).then_inc(ident_ready, 1)
            pool.wait_ge(ident_ready, 1)
            nc.gpsimd.affine_select(out=ident[:, :], in_=ident[:, :], compare_op=ALU.not_equal, fill=1.0, base=0,
                                    pattern=[[-1, P]], channel_multiplier=1).then_inc(ident_ready, 1)
            nc.gpsimd.iota(rank[:, :], pattern=[[-1, NE]], base=NE, channel_multiplier=0,
                           allow_small_or_imprecise_dtypes=True).then_inc(const_ready, 1)
            nc.gpsimd.memset(half[:, :], -0.5).then_inc(const_ready, 1)
            pool.wait_ge(const_ready, 2)
            for i in (-2, -1, 0):
                pool_body(pool, i)
            with pool.Fori(1, B - 2) as i:
                pool_body(pool, i)
            for i in (B - 2, B - 1, B):
                pool_body(pool, i)

        def exp_scores(act, b, n):
            at_least(act, max_done, NT * b + n + 1)
            ps = s_ps[n % S_BANKS]
            nc.scalar.activation(ps[:, :], ps[:, :], ACT.Exp, bias=neg_max[:, n:n + 1], scale=-1.0,
                                 accum_out=den[:, n:n + 1]).then_inc(s_exp, 1)

        def exp_probs(act, b, n):
            at_least(act, st_done, NT * b + n + 1)
            at_least(act, pv_done, NT // 2 * b + n // 2 - P_BUFS // 2 + 1)
            nc.scalar.activation(prob[:, n % P_BUFS, :], st_ps[n % ST_BANKS][:, :], ACT.Exp, scale=-1.0).then_inc(p_done, 1)

        def log_sum(act, b, g):
            at_least(act, s_exp, NT * b + GT * (g + 1))
            nc.scalar.activation(ln_den[:, GT * g:GT * (g + 1)], den[:, GT * g:GT * (g + 1)], ACT.Ln).then_inc(ln_done, 1)

        def alpha_weights(act, b):
            at_least(act, alpha_in, b + 1)
            nc.scalar.activation(alpha[:, :, :], logit[:, :, :], ACT.Exp).then_inc(alpha_exp, 1)

        def gate_weights(act, b):
            at_least(act, gate_in, b + 1)
            nc.scalar.activation(ge[:, :, :], gd[:, :, :], ACT.Exp).then_inc(gate_exp, 1)

        def gelu(act, b, m):
            at_least(act, emptied[f"hid{m}"], b + 2)
            nc.scalar.activation(hid[:, m, :], hid[:, m, :], ACT.Gelu, bias=fb1_s[:, m:m + 1]).then_inc(hid_ready, 1)

        def act_body(act, i):
            for t in range(NT):
                b, n = lagged(i, t)
                if real(b):
                    exp_scores(act, b, n)
                if real(i):
                    exp_probs(act, i, t)
                for g in range(G):
                    for b in due(i, t, WHEN_A[f"ln{g}"]):
                        log_sum(act, b, g)
                for b in due(i, t, WHEN_A["gelu"]):
                    for m in range(M):
                        gelu(act, b, m)
                    act.preload_act_table_set(EXP_LN)
                for b in due(i, t, WHEN_A["gate"]):
                    gate_weights(act, b)
                for b in due(i, t, WHEN_A["alpha"]):
                    alpha_weights(act, b)

        @block.scalar
        def _(act):
            act.preload_act_table_set(EXP_LN)
            act.wait_ge(late_loaded, LATE_ALL)
            for i in (-2, -1, 0):
                act_body(act, i)
            with act.Fori(1, B - 2) as i:
                act_body(act, i)
            for i in (B - 2, B - 1, B):
                act_body(act, i)

        def links(dve, name, b, before=0):
            count = [before]

            def link(ins):
                count[0] += 1
                ins.then_inc(link_sem[name], 1)
                assert count[0] <= LINKS[name]

            def after():
                dve.wait_ge(link_sem[name], LINKS[name] * b + count[0])
            return link, after

        V = nc.vector

        def wide(small, n):
            return small.unsqueeze(2).to_broadcast([P, J, n])

        def row_max(dve, b, n):
            at_least(dve, s_done, NT * b + n + 1)
            V.tensor_reduce(neg_max[:, n:n + 1], s_ps[n % S_BANKS][:, :], AX.X, ALU.min).then_inc(max_done, 1)

        def rows_out(dve, b, n):
            at_least(dve, filled[f"e{n}_t"], b + 1)
            V.tensor_copy(rows_t[:, n, :], bank(f"e{n}_t")[0:EMB, :]).then_inc(emptied[f"e{n}_t"], 1)

        def proj_out(dve, b):
            at_least(dve, filled["proj"], b + 1)
            V.tensor_scalar(proj[:, :], bank("proj")[:, :], emb_b[:, 0:1], None, ALU.add).then_inc(emptied["proj"], 1)

        def logit_products(dve, b):
            link, after = links(dve, "alpha", b)
            at_least(dve, filled["proj_t"], b + 1)
            ps = bank("proj_t")[:, :].rearrange("p (k c) -> p k c", c=C)
            lflat = logit[:, :, :].rearrange("p j n -> p (j n)")
            link(V.tensor_tensor(lw[:, :, :], ps, wa[:, 0:C].unsqueeze(1).to_broadcast([P, 2 * J, C]), ALU.mult))
            after()
            link(V.tensor_reduce(lflat, lw[:, :, :], AX.X, ALU.add))

        def logit_offsets(dve, b):
            link, after = links(dve, "alpha", b, 2)
            lflat = logit[:, :, :].rearrange("p j n -> p (j n)")
            after()
            link(V.tensor_scalar(lflat, lflat, wa[:, C:C + 1], None, ALU.add))
            after()
            link(V.tensor_reduce(lmax[:, :], logit[:, :, :], AX.X, ALU.max))
            after()
            V.tensor_tensor(logit[:, :, :], logit[:, :, :], wide(lmax[:, :], 2), ALU.subtract).then_inc(alpha_in, 1)

        def alpha_norm(dve, b):
            link, after = links(dve, "alpha", b, 4)
            at_least(dve, alpha_exp, b + 1)
            link(V.tensor_reduce(lsum[:, :], alpha[:, :, :], AX.X, ALU.add))
            after()
            link(V.reciprocal(lsum[:, :], lsum[:, :]))
            after()
            link(V.tensor_tensor(alpha[:, :, :], alpha[:, :, :], wide(lsum[:, :], 2), ALU.mult))

        def mix_embeddings(dve, b):
            link, after = links(dve, "alpha", b, 7)
            ps = bank("proj_t")[:, :].rearrange("p (k c) -> p k c", c=C)
            aflat = alpha[:, :, :].rearrange("p j n -> p (j n)").unsqueeze(2).to_broadcast([P, 2 * J, C])
            after()
            V.tensor_tensor(lw[:, :, :], ps, aflat, ALU.mult).then_inc(emptied["proj_t"], 1)

        def sum_embeddings(dve, b):
            link, after = links(dve, "alpha", b, 7)
            w4 = lw[:, :, :].rearrange("p (j n) c -> p j n c", n=2)
            h_b = h_all[:, b, :].rearrange("p (j c) -> p j c", c=C)
            at_least(dve, emptied["proj_t"], b + 2)
            link(V.tensor_tensor(h_b, w4[:, :, 0, :], w4[:, :, 1, :], ALU.add))
            link(V.tensor_tensor(h_now[:, :, :], w4[:, :, 0, :], w4[:, :, 1, :], ALU.add))

        def mean_of(dve, b, n):
            link, after = links(dve, f"ln{n + 1}", b)
            if n == 0:
                links(dve, "alpha", b, 9)[1]()
            else:
                at_least(dve, emptied["ctx_t"], b + 2)
            link(V.tensor_reduce(mean[n][:, :], (h_now, h1)[n][:, :, :], AX.X, ALU.add))
            after()
            link(V.tensor_scalar(mean[n][:, :], mean[n][:, :], 1.0 / C, None, ALU.mult))

        def centre(dve, b, n):
            link, after = links(dve, f"ln{n + 1}", b, 2)
            after()
            link(V.tensor_tensor(cent[n][:, :, :], (h_now, h1)[n][:, :, :], wide(mean[n][:, :], C), ALU.subtract))
            after()
            link(V.tensor_tensor(sq[n][:, :, :], cent[n][:, :, :], cent[n][:, :, :], ALU.mult))

        def variance(dve, b, n):
            link, after = links(dve, f"ln{n + 1}", b, 4)
            after()
            link(V.tensor_reduce(var[n][:, :], sq[n][:, :, :], AX.X, ALU.add))
            after()
            V.tensor_scalar(var[n][:, :], var[n][:, :], 1.0 / C, EPS, ALU.mult, ALU.add).then_inc(var_ready[n], 1)

        def normalise(dve, b, n):
            link, after = links(dve, f"ln{n + 1}", b, 5)
            at_least(dve, rstd_ready[n], b + 1)
            link(V.tensor_tensor(sq[n][:, :, :], cent[n][:, :, :], wide(rstd[n][:, :], C), ALU.mult))
            after()
            link(V.tensor_copy(xs[n][:, :, 0:C], sq[n][:, :, :]))

        def low_part(dve, b, n):
            links(dve, f"ln{n + 1}", b, 7)[1]()
            V.tensor_tensor(xs[n][:, :, C:2 * C], sq[n][:, :, :], xs[n][:, :, 0:C].bitcast(FP32), ALU.subtract).then_inc(xs_ready[n], 1)

        def x_out(dve, b, n):
            name = ("x_t", "x2_t")[n]
            at_least(dve, filled[name], b + 1)
            V.tensor_copy(xt[n][:, :], bank(name)[:, :]).then_inc(emptied[name], 1)

        def split_high(dve, b, g, which):
            name = f"{which}{g}"
            raw, scale = (raw_q, -1.0 / C ** 0.5) if which == "q" else (raw_k, 1.0)
            at_least(dve, filled[name], b + 1)
            if which == "q":
                for h in range(g * HG, (g + 1) * HG):
                    at_least(dve, stacked[h], STACK * b)
            V.tensor_scalar(raw[g][:, 0, :], bank(name)[:, :], scale, None, ALU.mult).then_inc(high_ready[name], 1)

        def split_low(dve, b, g, which):
            name = f"{which}{g}"
            raw, scale = (raw_q, -1.0 / C ** 0.5) if which == "q" else (raw_k, 1.0)
            dve.wait_ge(high_ready[name], b + 1)
            V.scalar_tensor_tensor(raw[g][:, 1, :], bank(name)[:, :], scale, raw[g][:, 0, :].bitcast(FP32), ALU.mult, ALU.subtract).then_inc(emptied[name], 1)

        def v_out(dve, b, g, part):
            name = f"v{g}" + "ab"[part]
            at_least(dve, filled[name], b + 1)
            if part == 0:
                for h in range(g * HG, (g + 1) * HG):
                    at_least(dve, v_stored[h], b)
            V.tensor_copy(raw_v[g][:, 2 * part:2 * part + 2, :].rearrange("p j c -> p (j c)"), bank(name)[:, :]).then_inc(emptied[name], 1)

        def shift_parts(dve, b, g):
            at_least(dve, ln_done, G * b + g + 1)
            cols = slice(GT * g, GT * (g + 1))
            ld = ln_den[:, cols].rearrange("p (h j) -> p j h", j=J)
            nm = neg_max[:, cols].rearrange("p (h j) -> p j h", j=J)
            V.tensor_tensor(shift[:, :, :], ld, nm, ALU.subtract).then_inc(link_sem["row"], 1)
            dve.wait_ge(link_sem["row"], 4 * b + 2 * g + 1)
            V.tensor_copy(shift_s[:, :, 0, :], shift[:, :, :]).then_inc(link_sem["row"], 1)
            dve.wait_ge(link_sem["row"], 4 * b + 2 * g + 2)
            V.tensor_tensor(shift_s[:, :, 1, :], shift[:, :, :], shift_s[:, :, 0, :].bitcast(FP32), ALU.subtract).then_inc(shift_ready, 1)

        def shift_out(dve, b, g):
            at_least(dve, filled[f"row{g}"], b + 1)
            if g == 0:
                at_least(dve, shift_stored[1], 32 * b)
            else:
                at_least(dve, shift_stored[0], 32 * (b + 1))
            V.tensor_copy(shift_t[:, :], bank(f"row{g}")[0:2 * HG, :]).then_inc(emptied[f"row{g}"], 1)

        def ctx_out(dve, b):
            at_least(dve, pv_done, NT // 2 * (b + 1))
            V.tensor_copy(ctx_s[:, :], ctx_ps[:, :]).then_inc(ctx_read, 1)

        def add_attention(dve, b):
            link, after = links(dve, "h1", b)
            at_least(dve, filled["ctx_t"], b + 1)
            ps = bank("ctx_t")[:, :].rearrange("p (j c) -> p j c", j=J)
            h_b = h_all[:, b, :].rearrange("p (j c) -> p j c", c=C)
            dve.wait_ge(res_ready, J * (b + 1))
            link(V.tensor_tensor(h1[:, :, :], ps[:, :, 0:C], h_b, ALU.add))
            after()
            V.tensor_tensor(h1[:, :, :], ps[:, :, C:2 * C], h1[:, :, :], ALU.add).then_inc(emptied["ctx_t"], 1)

        def hidden_out(dve, b, m):
            at_least(dve, filled[f"hid{m}"], b + 1)
            V.tensor_copy(hid[:, m, :], bank(f"hid{m}")[:, :]).then_inc(emptied[f"hid{m}"], 1)

        def gate_logits(dve, b):
            link, after = links(dve, "gate", b)
            at_least(dve, filled["gate"], b + 1)
            ps = bank("gate")[:, 0:J * NE].rearrange("p (j e) -> p j e", e=NE)
            V.tensor_tensor(gl[:, :, :], ps, bg_bd_s[:, 0:NE].unsqueeze(1).to_broadcast([P, J, NE]), ALU.add).then_inc(emptied["gate"], 1)
            at_least(dve, emptied["gate"], b + 2)
            link(V.tensor_reduce(gmax[:, :], gl[:, :, :], AX.X, ALU.max))
            after()
            V.tensor_tensor(gd[:, :, :], gl[:, :, :], wide(gmax[:, :], NE), ALU.subtract).then_inc(gate_in, 1)

        def rank_tops(dve, b):
            link, after = links(dve, "gate", b, 1)
            at_least(dve, gate_in, b + 1)
            link(V.tensor_scalar(geq[:, :, :], gd[:, :, :], 0.0, None, ALU.is_ge))
            after()
            link(V.tensor_tensor(geq[:, :, :], geq[:, :, :], rank[:, :].unsqueeze(1).to_broadcast([P, J, NE]), ALU.mult))
            after()
            link(V.tensor_reduce(gtop[:, :], geq[:, :, :], AX.X, ALU.max))
            after()
            link(V.tensor_tensor(geq[:, :, :], geq[:, :, :], wide(gtop[:, :], NE), ALU.is_equal))

        def route(dve, b):
            link, after = links(dve, "gate", b, 5)
            at_least(dve, gate_exp, b + 1)
            link(V.tensor_reduce(gsum[:, :], ge[:, :, :], AX.X, ALU.add))
            after()
            link(V.reciprocal(gp[:, :], gsum[:, :]))
            after()
            V.tensor_tensor(coef[:, :, :], geq[:, :, :], wide(gp[:, :], NE), ALU.mult).then_inc(coef_ready, 1)

        def y_out(dve, b, j):
            at_least(dve, filled[f"y{j}"], b + 1)
            if j >= 2:
                if not isinstance(b, int) or b < B - 1:
                    at_least(dve, res_ready, J * (b + 1) + j - 1)
                elif j % 2 == 0:
                    at_least(dve, res_ready, J * (b + 1) + j // 2)
                else:
                    dve.wait_ge(tail_mixed, j // 2)
            V.tensor_tensor(yb[:, j % 2, :, :].rearrange("p e c -> p (e c)"), bank(f"y{j}")[:, :], bg_bd_s[:, NE:], ALU.add).then_inc(emptied[f"y{j}"], 1)

        def tail_mix(dve, j):
            y = yb[:, j % 2, :, :]
            steps = 4 * (j // 2)
            dve.wait_ge(emptied[f"y{j}"], B + 1)
            if j == 1:
                dve.wait_ge(coef_ready, B)
                dve.wait_ge(out_stored, 16 * B)
            V.tensor_tensor(y, y, coef[:, j, :].unsqueeze(2).to_broadcast([P, NE, C]), ALU.mult).then_inc(tail_step, 1)
            dve.wait_ge(tail_step, steps + 1)
            V.tensor_tensor(yb[:, j % 2, 0:4, :], yb[:, j % 2, 0:4, :], yb[:, j % 2, 4:8, :], ALU.add).then_inc(tail_step, 1)
            dve.wait_ge(tail_step, steps + 2)
            V.tensor_tensor(yb[:, j % 2, 0:2, :], yb[:, j % 2, 0:2, :], yb[:, j % 2, 2:4, :], ALU.add).then_inc(tail_step, 1)
            dve.wait_ge(tail_step, steps + 3)
            V.tensor_tensor(yb[:, j % 2, 0, :], yb[:, j % 2, 0, :], yb[:, j % 2, 1, :], ALU.add).then_inc(tail_step, 1)
            dve.wait_ge(tail_step, steps + 4)
            V.tensor_tensor(res[:, j, :], yb[:, j % 2, 0, :], h1[:, j, :], ALU.add).then_inc(tail_mixed, 1)

        def vector_body(dve, i):
            for t in range(NT):
                b, n = s_tile(i, t)
                if real(b):
                    row_max(dve, b, n)
                for n in range(2):
                    for b in due(i, t, WHEN_V[f"e{n}_t"]):
                        rows_out(dve, b, n)
                for b in due(i, t, WHEN_V["proj"]):
                    proj_out(dve, b)
                for b in due(i, t, WHEN_V["logits"]):
                    logit_products(dve, b)
                for b in due(i, t, WHEN_V["logits"] + 1):
                    logit_offsets(dve, b)
                for b in due(i, t, WHEN_V["alpha"]):
                    alpha_norm(dve, b)
                for b in due(i, t, WHEN_V["alpha"] + 1):
                    mix_embeddings(dve, b)
                for b in due(i, t, WHEN_V["alpha"] + 2):
                    sum_embeddings(dve, b)
                for b in due(i, t, WHEN_V["ctx"]):
                    ctx_out(dve, b)
                for b in due(i, t, WHEN_V["h1"]):
                    add_attention(dve, b)
                for n, at in ((0, WHEN_V["layer0"]), (1, WHEN_V["layer1"])):
                    for b in due(i, t, at):
                        mean_of(dve, b, n)
                    for b in due(i, t, at + 1):
                        centre(dve, b, n)
                    for b in due(i, t, at + 2):
                        variance(dve, b, n)
                for n in range(2):
                    for b in due(i, t, WHEN_V[f"normal{n}"]):
                        normalise(dve, b, n)
                    for b in due(i, t, WHEN_V[f"normal{n}"] + 1):
                        low_part(dve, b, n)
                    for b in due(i, t, WHEN_V[("x_t", "x2_t")[n]]):
                        x_out(dve, b, n)
                for m in range(M):
                    for b in due(i, t, WHEN_V[f"hid{m}"]):
                        hidden_out(dve, b, m)
                for b in due(i, t, WHEN_V["gate"]):
                    gate_logits(dve, b)
                for b in due(i, t, WHEN_V["tops"]):
                    rank_tops(dve, b)
                for b in due(i, t, WHEN_V["route"]):
                    route(dve, b)
                for j in range(J):
                    for b in due(i, t, WHEN_V[f"y{j}"]):
                        y_out(dve, b, j)
                        if j % 2 and isinstance(b, int) and b == B - 1:
                            tail_mix(dve, j)
                for g in range(G):
                    for b in due(i, t, WHEN_V[f"parts{g}"]):
                        shift_parts(dve, b, g)
                    for b in due(i, t, WHEN_V[f"row{g}"]):
                        shift_out(dve, b, g)
                    for which in "qk":
                        at = WHEN_V[f"{which}{g}"]
                        for b in due(i, t, at):
                            split_high(dve, b, g, which)
                        for b in due(i, t, at + 1):
                            split_low(dve, b, g, which)
                    for part in range(2):
                        for b in due(i, t, WHEN_V[f"v{g}" + "ab"[part]]):
                            v_out(dve, b, g, part)

        @block.vector
        def _(dve):
            V.memset(kst[3 * R:3 * R + 2, :, :].bitcast(FP32), 1.0).then_inc(ones_ready, 1)
            dve.wait_ge(w_loaded, W_ALL)
            V.tensor_copy(w_hi[:, :], w_raw[:, :]).then_inc(w_split, 1)
            dve.wait_ge(w_split, 1)
            V.tensor_tensor(w_lo[:, :], w_raw[:, :], w_hi[:, :].bitcast(FP32), ALU.subtract).then_inc(w_split, 1)
            dve.wait_ge(emb_loaded, EMB_ALL)
            for i in (-2, -1, 0):
                if i == 0:
                    dve.wait_ge(late_loaded, LATE_ALL)
                    dve.wait_ge(const_ready, 2)
                vector_body(dve, i)
            with dve.Fori(1, B - 2) as i:
                vector_body(dve, i)
            for i in (B - 2, B - 1, B):
                vector_body(dve, i)

        PE = nc.tensor

        def claim(pe, i, name):
            at = POS[name] - SH_BANKS
            body = i
            for _ in range(3 * len(SHARED)):
                if at < 0:
                    at += len(SHARED)
                    body = body - 1
                prev, rel = SHARED[at]
                if real(body + rel):
                    at_least(pe, emptied[prev], body + rel + 2)
                    return
                at -= SH_BANKS

        def scores(pe, b, n):
            h, c = divmod(n, J)
            if c == 0:
                pe.wait_ge(stacked[h], STACK * (b + 1))
            if n < S_BANKS:
                last = max(m for m in range(NT) if m % S_BANKS == n)
                at_least(pe, s_exp, NT * (b - 1) + last + 1)
            else:
                at_least(pe, s_exp, NT * b + n - S_BANKS + 1)
            PE.matmul(s_ps[n % S_BANKS][:, :], qst[0:3 * R, h, c * P:(c + 1) * P], kst[0:3 * R, h, :],
                      start=True, stop=True).then_inc(s_done, 1)

        def scores_t(pe, b, n):
            h, c = divmod(n, J)
            if n % GT == 0:
                pe.wait_ge(shift_stored[n // GT], 32 * (b + 1))
            at_least(pe, p_done, NT * b + n - ST_BANKS + 1)
            PE.matmul(st_ps[n % ST_BANKS][:, :], kst[:, h, c * P:(c + 1) * P], qst[:, h, :],
                      start=True, stop=True).then_inc(st_done, 1)

        def context(pe, b, pair):
            h, c = divmod(2 * pair, J)
            if c == 0:
                pe.wait_ge(v_stored[h], b + 1)
            if pair == 0:
                at_least(pe, ctx_read, b)
            pe.wait_ge(p_done, NT * b + 2 * pair + 2)
            for d in range(2):
                last = PE.matmul(ctx_ps[d * C:(d + 1) * C, :], val[:, h, c + d, :], prob[:, (2 * pair + d) % P_BUFS, :],
                                 start=(pair == 0), stop=(pair == NT // 2 - 1))
            last.then_inc(pv_done, 1)

        def transposes(pe, i, name, pieces, rows_):
            claim(pe, i, name)
            for j, piece in enumerate(pieces):
                last = PE.transpose(bank(name)[0:rows_, j * P:(j + 1) * P], piece, ident[:, :])
            last.then_inc(filled[name], 1)

        def embed_t(pe, i, b, n):
            if n == 0:
                at_least(pe, rows_loaded, 16 * J * (b + 1))
            transposes(pe, i, f"e{n}_t", [rows[:, j, n * EMB:(n + 1) * EMB] for j in range(J)], EMB)

        def embed_proj(pe, i, b):
            claim(pe, i, "proj")
            for n in range(2):
                at_least(pe, emptied[f"e{n}_t"], b + 2)
                last = PE.matmul(bank("proj")[n * C:(n + 1) * C, :], emb_w[:, n, :], rows_t[:, n, :], start=True, stop=True)
            last.then_inc(filled["proj"], 1)

        def two_pass(out_ap, parts, moving):
            PE.matmul(out_ap, parts[0], moving, start=True, stop=False)
            return PE.matmul(out_ap, parts[1], moving, start=False, stop=True)

        def project_qk(pe, i, b, g, which):
            name = f"{which}{g}"
            claim(pe, i, name)
            at_least(pe, emptied["x_t"], b + 2)
            o = (QO if which == "q" else KO) + g * P
            two_pass(bank(name)[:, :], (w_hi[:, o:o + P], w_lo[:, o:o + P]), xt[0][:, :]).then_inc(filled[name], 1)

        def project_v(pe, i, b, g, part):
            name = f"v{g}" + "ab"[part]
            claim(pe, i, name)
            at_least(pe, emptied["x_t"], b + 2)
            o = VO_ + g * HG * C
            for d in range(2):
                tok = slice((2 * part + d) * P, (2 * part + d + 1) * P)
                dst = bank(name)[:, d * HG * C:(d + 1) * HG * C]
                PE.matmul(dst, xt[0][:, tok], w_hi[:, o:o + HG * C], start=True, stop=False)
                last = PE.matmul(dst, xt[0][:, tok], w_lo[:, o:o + HG * C], start=False, stop=True)
            last.then_inc(filled[name], 1)

        def shift_row(pe, i, b, g):
            at_least(pe, shift_ready, G * b + g + 1)
            transposes(pe, i, f"row{g}", [shift_s[:, j, :, :].bitcast(FP32).rearrange("p a h -> p (a h)") for j in range(J)], 2 * HG)

        def hidden(pe, i, b, m):
            name = f"hid{m}"
            claim(pe, i, name)
            at_least(pe, emptied["x2_t"], b + 2)
            o = FO + m * P
            two_pass(bank(name)[:, :], (w_hi[:, o:o + P], w_lo[:, o:o + P]), xt[1][:, :]).then_inc(filled[name], 1)

        def gate(pe, i, b, j):
            if j == 0:
                claim(pe, i, "gate")
                at_least(pe, hid_ready, M * (b + 1))
            for m in range(M):
                last = PE.matmul(bank("gate")[:, j * NE:(j + 1) * NE], hid[:, m, j * P:(j + 1) * P], wg[:, m, :],
                                 start=(m == 0), stop=(m == M - 1))
            if j == J - 1:
                last.then_inc(filled["gate"], 1)

        def experts(pe, i, b, j, m):
            name = f"y{j}"
            if m == 0:
                claim(pe, i, name)
            last = PE.matmul(bank(name)[:, :], hid[:, m, j * P:(j + 1) * P], wd[:, m, :], start=(m == 0), stop=(m == M - 1))
            if m == M - 1:
                last.then_inc(filled[name], 1)

        def tensor_body(pe, i):
            for t in range(NT):
                b, n = s_tile(i, t)
                if real(i):
                    scores_t(pe, i, t)
                if real(b):
                    scores(pe, b, n)
                if t % 2 == 0 and t < LAG_PV and real(i - 1):
                    context(pe, i - 1, (NT - LAG_PV + t) // 2)
                if t % 2 == 0 and t >= LAG_PV and real(i):
                    context(pe, i, (t - LAG_PV) // 2)
                for b in due(i, t, WHEN_T["ctx_t"]):
                    at_least(pe, ctx_read, b + 1)
                    transposes(pe, i, "ctx_t", [ctx_s[:, j * P:(j + 1) * P] for j in range(J)], P)
                for b in due(i, t, WHEN_T["x2_t"]):
                    at_least(pe, xs_ready[1], b + 1)
                    transposes(pe, i, "x2_t", [xs[1][:, j, :].bitcast(FP32) for j in range(J)], P)
                for g in range(G):
                    for b in due(i, t, WHEN_T[f"row{g}"]):
                        shift_row(pe, i, b, g)
                for m in range(M):
                    for b in due(i, t, WHEN_T[f"hid{m}"]):
                        hidden(pe, i, b, m)
                for j in range(J):
                    for b in due(i, t, WHEN_T["gate"] + j):
                        gate(pe, i, b, j)
                for g in range(G):
                    for which in "qk":
                        for b in due(i, t, WHEN_T[f"{which}{g}"]):
                            project_qk(pe, i, b, g, which)
                    for part in range(2):
                        for b in due(i, t, WHEN_T[f"v{g}" + "ab"[part]]):
                            project_v(pe, i, b, g, part)
                for n in range(2):
                    for b in due(i, t, WHEN_T[f"e{n}_t"]):
                        embed_t(pe, i, b, n)
                for b in due(i, t, WHEN_T["proj"]):
                    embed_proj(pe, i, b)
                for b in due(i, t, WHEN_T["proj_t"]):
                    at_least(pe, emptied["proj"], b + 2)
                    transposes(pe, i, "proj_t", [proj[:, j * P:(j + 1) * P] for j in range(J)], P)
                for j in range(J):
                    for m in range(M):
                        for b in due(i, t, WHEN_T[f"y{j}"] + m):
                            experts(pe, i, b, j, m)
                for b in due(i, t, WHEN_T["x_t"]):
                    at_least(pe, xs_ready[0], b + 1)
                    transposes(pe, i, "x_t", [xs[0][:, j, :].bitcast(FP32) for j in range(J)], P)

        @block.tensor
        def _(pe):
            pe.wait_ge(ident_ready, 2)
            pe.wait_ge(emb_loaded, EMB_ALL)
            for i in (-2, -1, 0):
                if i == -1:
                    pe.wait_ge(w_split, 2)
                if i == 0:
                    pe.wait_ge(ones_ready, 1)
                    pe.wait_ge(late_loaded, LATE_ALL)
                tensor_body(pe, i)
            with pe.Fori(1, B - 2) as i:
                tensor_body(pe, i)
            for i in (B - 2, B - 1, B):
                tensor_body(pe, i)


def kernel(x, L0_tok_E0, L0_tok_E1, L0_tok_W0, L0_tok_b0, L0_tok_W1, L0_tok_b1, L0_tok_Wa, L0_tok_ba,
           L0_attn_Q, L0_attn_K, L0_attn_VO, L0_ffn_W1, L0_ffn_b1, L0_ffn_Wg, L0_ffn_bg, L0_ffn_Wd, L0_ffn_bd):
    import concourse.bacc as bacc
    from concourse.bass_utils import run_bass_kernel_spmd

    a = np.ascontiguousarray
    weights = [np.asarray(L0_attn_Q).reshape(H * R, C).T, np.asarray(L0_attn_K).reshape(H * R, C).T,
               np.asarray(L0_attn_VO).transpose(1, 0, 2).reshape(C, H * C), np.asarray(L0_ffn_W1)]
    arrays = {
        "tokens": a(x),
        "emb": a(np.concatenate([np.asarray(L0_tok_E0), np.asarray(L0_tok_E1)], axis=1)),
        "emb_W": a(np.stack([np.asarray(L0_tok_W0), np.asarray(L0_tok_W1)], axis=1)),
        "emb_B": a(np.concatenate([np.asarray(L0_tok_b0).reshape(C, 1), np.asarray(L0_tok_b1).reshape(C, 1)])),
        "wa_ba": a(np.concatenate([np.asarray(L0_tok_Wa).reshape(1, C), np.asarray(L0_tok_ba).reshape(1, 1)], axis=1)),
        "weights": a(np.concatenate(weights, axis=1)),
        "fb1": a(np.asarray(L0_ffn_b1).reshape(M, P).T),
        "Wg": a(L0_ffn_Wg),
        "bg_bd": a(np.concatenate([np.asarray(L0_ffn_bg).reshape(1, NE), np.asarray(L0_ffn_bd).reshape(1, NE * C)], axis=1)),
        "WdT": a(np.asarray(L0_ffn_Wd).transpose(1, 0, 2).reshape(HID, NE * C)),
    }
    nc = bacc.Bacc("TRN2", target_bir_lowering=False, num_devices=1)
    aps = {n: nc.dram_tensor(n, v.shape, mybir.dt.from_np(v.dtype), kind="ExternalInput").ap() for n, v in arrays.items()}
    out = nc.dram_tensor("out", (B, T, C), FP32, kind="ExternalOutput").ap()
    lm_tower(nc, out=out, **aps)
    r = run_bass_kernel_spmd(nc, [arrays], core_ids=[0])
    return r.results[0]["out"]
```
